# Optimizing a Trainium2 kernel written in Bass

```python
import numpy as np
import jax
import jax.numpy as jnp

def _softmax(x, axis=-1):
    return jax.nn.softmax(x, axis=axis)

def _gelu(x):
    return jax.nn.gelu(x, approximate=True)

def _silu(x):
    return jax.nn.silu(x)

def _sigmoid(x):
    return jax.nn.sigmoid(x)

def _layernorm(x, axis=-1, eps=1e-05):
    m = jnp.mean(x, axis=axis, keepdims=True)
    v = jnp.var(x, axis=axis, keepdims=True)
    return (x - m) / jnp.sqrt(v + eps)

def _scatter_add(tgt, idx, src, axis=0):
    return tgt.at[idx].add(src)

def _segment_sum(src, seg, n):
    return jax.ops.segment_sum(src, seg, n)
kernel_name = 'mk_flamingo_gated_d1_seqx_r8_0f1e99'

def setup_inputs(seed: int=0):
    np.random.seed(seed)
    _w = jnp.asarray

    def _rec_inputs():
        import jax
        import jax.numpy as jnp
        _rk = jax.random.key(seed)
        x = -0.0002928 + 1 * jax.random.normal(jax.random.fold_in(_rk, 1), (16, 128, 128), jnp.float32)
        _lenS = 128 - jax.random.randint(jax.random.fold_in(_rk, 7), (16,), 0, max(1, 128 // 4) + 1, jnp.int32)
        _lenS2 = 128 - jax.random.randint(jax.random.fold_in(_rk, 8), (16,), 0, max(1, 128 // 4) + 1, jnp.int32)
        _ctx_1024P = jax.random.normal(jax.random.fold_in(_rk, 11), (16, 16, 128), jnp.float32)
        _ctx_1024c = jax.random.dirichlet(jax.random.fold_in(_rk, 511), 0.3 * jnp.ones((16,), jnp.float32), (16, 128))
        _ctx_1024t = jnp.einsum('bsk,bkd->bsd', _ctx_1024c, _ctx_1024P)
        _ctx_1024t = _ctx_1024t * jax.lax.rsqrt(jnp.mean(jnp.square(_ctx_1024t)) + 1e-12) * 0.953939
        ctx_1024 = -1.39393e-06 + 0.999914 * (_ctx_1024t + 0.3 * jax.random.normal(jax.random.fold_in(_rk, 611), (16, 128, 128), jnp.float32))
        _validS = jnp.arange(128)[None, :] < _lenS[:, None]
        _validS2 = jnp.arange(128)[None, :] < _lenS2[:, None]
        _causal = jnp.tril(jnp.ones((128, 128), dtype=bool))
        mask_SxS2_bk0 = jnp.logical_not(jnp.broadcast_to(_validS2[0:1, :], (128, 128)))
        _g = jax.random.normal(jax.random.fold_in(_rk, 9001), (2, 1), jnp.float32)
        _g = jnp.sign(_g) * jnp.maximum(jnp.abs(_g), 1.0) + (_g == 0) * 1.0
        g_xattn = _g[0]
        g_ffn = _g[1]
        return (x, ctx_1024, mask_SxS2_bk0, g_xattn, g_ffn)
    x, ctx_1024, mask_SxS2_bk0, g_xattn, g_ffn = _rec_inputs()

    def _L0_xattn_setup():
        import jax, jax.numpy as jnp
        import numpy as np
        D_MODEL = 128
        N_HEADS = 16
        D_HEAD = D_MODEL // N_HEADS
        B, S = (2, 256)
        key = jax.random.key(seed)
        ks = jax.random.split(key, 7)
        query = jax.random.normal(ks[0], (B, S, D_MODEL), dtype=jnp.float32)
        k_in = jax.random.normal(ks[1], (B, S, D_MODEL), dtype=jnp.float32)
        v_in = jax.random.normal(ks[2], (B, S, D_MODEL), dtype=jnp.float32)
        mask = jnp.tril(jnp.ones((S, S), dtype=bool))
        scale = 1.0 / np.sqrt(D_MODEL)
        Wq = jax.random.normal(ks[3], (D_MODEL, D_MODEL), dtype=jnp.float32) * scale
        Wk = jax.random.normal(ks[4], (D_MODEL, D_MODEL), dtype=jnp.float32) * scale
        Wv = jax.random.normal(ks[5], (D_MODEL, D_MODEL), dtype=jnp.float32) * scale
        Wo = jax.random.normal(ks[6], (D_MODEL, D_MODEL), dtype=jnp.float32) * scale
        return {'query': query, 'key': k_in, 'value': v_in, 'mask': mask, 'Wq': Wq, 'Wk': Wk, 'Wv': Wv, 'Wo': Wo}
    _L0_xattn_all = _L0_xattn_setup()
    _L0_xattn_in = {k: v for k, v in _L0_xattn_all.items() if k in ('Wq', 'Wk', 'Wv', 'Wo')}
    del _L0_xattn_all

    def _L0_ffn_setup():
        import jax, jax.numpy as jnp
        import numpy as np
        B, S, H, E, K = (2, 128, 128, 8, 2)
        F = 4 * H
        key = jax.random.key(seed)
        ks = jax.random.split(key, 8)
        std = 0.02
        return {'x': jax.random.normal(ks[0], (B, S, H), jnp.float32), 'gate_w': jax.random.normal(ks[1], (E, H), jnp.float32) * (std / np.sqrt(H)), 'gate_bias': jnp.zeros((E,), jnp.float32), 'Wu': jax.random.normal(ks[2], (E, F, H), jnp.float32) * std, 'bu': jnp.zeros((E, F), jnp.float32), 'Wd': jax.random.normal(ks[3], (E, H, F), jnp.float32) * std, 'bd': jnp.zeros((E, H), jnp.float32), 'sWu': jax.random.normal(ks[4], (F, H), jnp.float32) * std, 'sbu': jnp.zeros((F,), jnp.float32), 'sWd': jax.random.normal(ks[5], (H, F), jnp.float32) * std, 'sbd': jnp.zeros((H,), jnp.float32)}
    _L0_ffn_all = _L0_ffn_setup()
    _L0_ffn_in = {k: v for k, v in _L0_ffn_all.items() if k in ('gate_w', 'gate_bias', 'Wu', 'bu', 'Wd', 'bd', 'sWu', 'sbu', 'sWd', 'sbd')}
    del _L0_ffn_all
    return {'x': x, 'ctx_1024': ctx_1024, 'mask_SxS2_bk0': mask_SxS2_bk0, 'g_xattn': g_xattn, 'g_ffn': g_ffn, 'L0_xattn_Wq': _L0_xattn_in['Wq'], 'L0_xattn_Wk': _L0_xattn_in['Wk'], 'L0_xattn_Wv': _L0_xattn_in['Wv'], 'L0_xattn_Wo': _L0_xattn_in['Wo'], 'L0_ffn_gate_w': _L0_ffn_in['gate_w'], 'L0_ffn_gate_bias': _L0_ffn_in['gate_bias'], 'L0_ffn_Wu': _L0_ffn_in['Wu'], 'L0_ffn_bu': _L0_ffn_in['bu'], 'L0_ffn_Wd': _L0_ffn_in['Wd'], 'L0_ffn_bd': _L0_ffn_in['bd'], 'L0_ffn_sWu': _L0_ffn_in['sWu'], 'L0_ffn_sbu': _L0_ffn_in['sbu'], 'L0_ffn_sWd': _L0_ffn_in['sWd'], 'L0_ffn_sbd': _L0_ffn_in['sbd']}

def reference(x, ctx_1024, mask_SxS2_bk0, g_xattn, g_ffn, L0_xattn_Wq, L0_xattn_Wk, L0_xattn_Wv, L0_xattn_Wo, L0_ffn_gate_w, L0_ffn_gate_bias, L0_ffn_Wu, L0_ffn_bu, L0_ffn_Wd, L0_ffn_bd, L0_ffn_sWu, L0_ffn_sbu, L0_ffn_sWd, L0_ffn_sbd):
    import jax
    import jax.numpy as jnp

    def _L0_xattn_ref(query, key, value, mask, Wq, Wk, Wv, Wo):
        import jax, jax.numpy as jnp
        import numpy as np
        D_MODEL = 128
        N_HEADS = 16
        D_HEAD = D_MODEL // N_HEADS
        B, S = (2, 256)
        b, sq, d = query.shape
        q = (query @ Wq.T).reshape(b, sq, N_HEADS, D_HEAD).transpose(0, 2, 1, 3)
        k = (key @ Wk.T).reshape(b, -1, N_HEADS, D_HEAD).transpose(0, 2, 1, 3)
        v = (value @ Wv.T).reshape(b, -1, N_HEADS, D_HEAD).transpose(0, 2, 1, 3)
        scores = jnp.einsum('bhqd,bhkd->bhqk', q, k) / jnp.sqrt(jnp.float32(D_HEAD))
        scores = jnp.where(mask[None, None, :, :], scores, jnp.float32(-1000000000.0))
        attn = jax.nn.softmax(scores, axis=-1)
        ctx = jnp.einsum('bhqk,bhkd->bhqd', attn, v)
        ctx = ctx.transpose(0, 2, 1, 3).reshape(b, sq, d)
        return ctx @ Wo.T

    def _L0_ffn_ref(x, gate_w, gate_bias, Wu, bu, Wd, bd, sWu, sbu, sWd, sbd):
        import jax, jax.numpy as jnp
        import numpy as np
        B, S, H, E, K = (2, 128, 128, 8, 2)
        F = 4 * H
        b, s, h = x.shape
        x_flat = x.reshape(-1, h)
        T = x_flat.shape[0]
        scores = jax.nn.sigmoid(x_flat @ gate_w.T + gate_bias)
        top_scores, top_idx = jax.lax.top_k(scores, K)
        top_scores = top_scores / (top_scores.sum(-1, keepdims=True) + 1e-06)
        w = jnp.zeros((T, E), x.dtype).at[jnp.arange(T)[:, None], top_idx].add(top_scores)
        h1 = jnp.einsum('th,efh->etf', x_flat, Wu) + bu[:, None, :]
        a1 = jax.nn.gelu(h1, approximate=False)
        y = jnp.einsum('etf,ehf->eth', a1, Wd) + bd[:, None, :]
        combined = jnp.einsum('te,eth->th', w, y)
        sh = jax.nn.gelu(x_flat @ sWu.T + sbu, approximate=False)
        shared = (sh @ sWd.T + sbd) * 0.1
        return (combined + shared).reshape(b, s, h)
    x = x + jnp.tanh(g_xattn[0]) * _L0_xattn_ref(_layernorm(x, axis=-1), ctx_1024, ctx_1024, mask_SxS2_bk0, L0_xattn_Wq, L0_xattn_Wk, L0_xattn_Wv, L0_xattn_Wo)
    x = x + jnp.tanh(g_ffn[0]) * _L0_ffn_ref(_layernorm(x, axis=-1), L0_ffn_gate_w, L0_ffn_gate_bias, L0_ffn_Wu, L0_ffn_bu, L0_ffn_Wd, L0_ffn_bd, L0_ffn_sWu, L0_ffn_sbu, L0_ffn_sWd, L0_ffn_sbd)
    return x

_drawn_inputs = setup_inputs


def setup_inputs(seed=0):
    import zlib

    import numpy as np

    out = dict(_drawn_inputs(seed))
    spreads = {'L0_ffn_gate_bias': (0.0, 0.1),
     'L0_ffn_bu': (0.0, 0.551),
     'L0_ffn_bd': (0.0, 0.1),
     'L0_ffn_sbu': (0.0, 0.8),
     'L0_ffn_sbd': (0.0, 0.8)}
    factors = {'L0_ffn_sWu': 8.0, 'L0_ffn_sWd': 8.0}
    for name, (base, spread) in spreads.items():
        noise = np.random.default_rng([zlib.crc32(name.encode()), seed]).standard_normal(out[name].shape)
        drawn = base * np.exp(spread * noise) if base else spread * noise
        out[name] = jnp.asarray(drawn.astype(out[name].dtype))
    for name, factor in factors.items():
        out[name] = (out[name] * factor).astype(out[name].dtype)
    return out
```

```python
from contextlib import ExitStack

import concourse.bass as bass
import concourse.mybir as mybir
import numpy as np


def build(nc, x_in, ctxT_in, mask_in, g_x_in, g_f_in, wqkvo_in, wffn_in, bu_in, bd_in, gate_wT_in, gate_b_in,
          ident_in, earlier_in, out_dram):
    f32, f32r, bf16, fp16, u8 = (mybir.dt.float32, mybir.dt.float32r, mybir.dt.bfloat16, mybir.dt.float16,
                                 mybir.dt.uint8)
    ALU, ACT, AX = mybir.AluOpType, mybir.ActivationFunctionType, mybir.AxisListType

    NB, SEQ, D = x_in.shape
    HEADS, DH = 16, D // 16
    E1 = wffn_in.shape[1] // 2
    E = E1 - 1
    GB = 4
    NG = NB // GB
    TOK = GB * SEQ
    HU = 4
    UB = HEADS // HU
    UN = GB * UB
    PARTS = 4
    VC = 3 * DH + 1
    FC = wffn_in.shape[2] // D
    CH = E1 * FC
    EPS, MASKED, TINY = 1e-5, 1e9, 1e-6
    QSCALE = float(1.0 / np.sqrt(np.float32(DH)))
    SHARED_WEIGHT = 0.1

    qk_dram = nc.dram_tensor("qk_dram", (4, D, NB * SEQ), f32, kind="Internal").ap()
    w_dram = nc.dram_tensor("w_dram", (NG, E, TOK), f32, kind="Internal").ap()

    ctx = ExitStack()
    with ctx:
        def sb(name, shape, dt):
            return ctx.enter_context(nc.sbuf_tensor(name, shape, dt))

        def sem(name):
            return ctx.enter_context(nc.semaphore(name))

        bank = [ctx.enter_context(nc.psum_tensor(f"bank{i}", [128, 512], f32)) for i in range(8)]

        identf = sb("identf", [128, 128], f32)
        identb = sb("identb", [128, 128], bf16)
        earlier = sb("earlier", [128, E * E], f32)
        ones = sb("ones", [128, 512], f32)
        minus_half = sb("minus_half", [128, GB], f32)
        e_const = sb("e_const", [128, GB * E], f32)
        mask8 = sb("mask8", [128, SEQ], u8)
        mask_bias = sb("mask_bias", [128, SEQ], bf16)
        row_open = sb("row_open", [128, 1], f32)
        gates = sb("gates", [128, 2], f32)
        tanh_gates = sb("tanh_gates", [128, 2], f32)
        wqkvo = sb("wqkvo", [128, 4 * D], f32)
        wqkvo_hi = sb("wqkvo_hi", [128, 4 * D], f32r)
        wqkvo_lo = sb("wqkvo_lo", [128, 4 * D], f32r)
        gate_w = sb("gate_w", [128, E], f32)
        gate_hi = sb("gate_hi", [128, E], f32r)
        gate_lo = sb("gate_lo", [128, E], f32r)
        gate_b = sb("gate_b", [128, E], f32)
        bu = sb("bu", [128, CH], f32)
        bd = sb("bd", [E1, D], f32)
        w_raw = sb("w_raw", [128, 2, 512], f32)
        w_hi = sb("w_hi", [128, 2 * E1, 512], f32r)
        w_lo = sb("w_lo", [128, 2 * E1, 512], f32r)

        x = sb("x", [128, NB, D], f32)
        ctxT = sb("ctxT", [128, NB * SEQ], f32)
        stats = sb("stats", [128, GB, 6], f32)
        mean_var = sb("mean_var", [128, GB, 2], f32)
        var_eps = sb("var_eps", [128, GB], f32)
        inv_std = sb("inv_std", [128, GB], f32)
        inv_std_open = sb("inv_std_open", [128, GB], f32)
        xn = sb("xn", [128, GB, D], f32)
        xnT_hi = sb("xnT_hi", [128, TOK], f32r)
        xnT_lo = sb("xnT_lo", [128, TOK], f32r)
        arena = sb("arena", [128, 4, NB * SEQ], f32r)
        act_hi = arena[:, 0, :].rearrange("p (s n) -> p s n", s=4)
        act_lo = arena[:, 1, :].rearrange("p (s n) -> p s n", s=4)
        ffnT_hi, ffnT_lo = arena[:, 2, :], arena[:, 3, :]
        v_parts = sb("v_parts", [128, NB, HEADS, VC], bf16)
        q_pack = sb("q_pack", [128, 2, UB, 2 * SEQ], f32r)
        cT_hi = q_pack[:, 0, 0:2, :].rearrange("p g t -> p (g t)")
        cT_lo = q_pack[:, 1, 0:2, :].rearrange("p g t -> p (g t)")
        k_pack = sb("k_pack", [128, 2, UB, HU, 2 * SEQ], f32r)
        neg_max = sb("neg_max", [128, 4, HU], f32)
        weight_all = k_pack[:, 0, :, :, :].rearrange("p g j k -> p (g j k)").bitcast(f32).rearrange(
            "p (e t) -> p e t", e=E)
        prob = sb("prob", [128, 2, HU, SEQ], f32)
        maskf, mask_low = prob[:, 0, 0, :], prob[:, 0, 1, :]
        v_rest = prob[:, 1, :, :].rearrange("p b (h d) -> p b h d", d=DH)
        y_scaled = prob[:, :, :, :].rearrange("p a b c -> p a (b c)")
        probT_hi = sb("probT_hi", [128, 2, HU * SEQ], fp16)
        probT_lo = sb("probT_lo", [128, 2, HU * SEQ], fp16)
        o_sum = sb("o_sum", [128, HEADS, DH], f32)
        inv_sum = sb("inv_sum", [128, HEADS], f32)
        o_norm = sb("o_norm", [128, 2, HEADS, DH], f32)
        oT_hi = sb("oT_hi", [128, 2, SEQ], f32r)
        oT_lo = sb("oT_lo", [128, 2, SEQ], f32r)
        neg_z = sb("neg_z", [128, GB, E], f32)
        exp_neg_z = sb("exp_neg_z", [128, GB, E], f32)
        sig_den = sb("sig_den", [128, GB, E], f32)
        sig = sb("sig", [128, GB, E], f32)
        compare = probT_hi[:, :, :].bitcast(f32).rearrange("p a (t e f) -> p a t e f", t=GB, e=E)
        beats, ties = compare[:, 0], compare[:, 1]
        rank = sb("rank", [128, GB, E], f32)
        sig_top = sb("sig_top", [128, GB, E], f32)
        top_sum = sb("top_sum", [128, GB], f32)
        inv_top = sb("inv_top", [128, GB], f32)
        weight = sb("weight", [128, GB, E1], f32)
        weightT = sb("weightT", [E1, TOK], f32)
        act = ctxT[:, :].rearrange("p (s n) -> p s n", s=4)
        moe = wqkvo[:, :]
        result = w_raw[:, 0, :].rearrange("p (b d) -> p b d", b=GB)

        s_mask, s_small, s_wa, s_x0, s_xrest = sem("mask_in"), sem("small_in"), sem("wa_in"), sem("x0_in"), sem("xrest_in")
        s_wraw = [sem("wraw_even"), sem("wraw_odd")]
        s_qk_out = sem("qk_out")
        s_pack = [sem("pack_even"), sem("pack_odd")]
        s_wt_out, s_wall, s_out = sem("weightT_out"), sem("weight_all_in"), sem("out")
        s_pool0, s_mk, s_wah, s_wal, s_tanh, s_ib = (sem("pool_constants"), sem("mask_done"), sem("wa_hi"), sem("wa_lo"),
                                                    sem("tanh_done"), sem("identb_done"))
        s_wh, s_wl = sem("ffn_w_hi"), sem("ffn_w_lo")
        s_mv, s_ve, s_pw, s_rs = sem("mean_var_p"), sem("var_eps_p"), sem("pow_p"), sem("inv_std_p")
        s_xn, s_xT, s_xh, s_xl = sem("xn_p"), sem("xnT_psum"), sem("xnT_hi"), sem("xnT_lo")
        s_ch, s_cl, s_q, s_k, s_v = sem("cT_hi"), sem("cT_lo"), sem("q_psum"), sem("k_psum"), sem("v_psum")
        s_qh, s_ql, s_kh, s_kl = sem("q_hi"), sem("q_lo"), sem("k_hi"), sem("k_lo")
        s_vh, s_vr, s_vm, s_vl = sem("v_high"), sem("v_rest"), sem("v_mid"), sem("v_low")
        s_s, s_mx, s_ex, s_t, s_ph, s_pl, s_pv = (sem("scores"), sem("neg_max"), sem("exps"), sem("probT"),
                                                  sem("probT_hi"), sem("probT_lo"), sem("pv"))
        s_os, s_on, s_oT, s_oh, s_ol, s_o, s_x2 = (sem("o_sum"), sem("o_norm"), sem("oT"), sem("oT_hi"), sem("oT_lo"),
                                                   sem("wo_out"), sem("residual"))
        s_mv2, s_ve2, s_rs2, s_xn2, s_xT2 = (sem("mean_var_f"), sem("var_eps_f"), sem("inv_std_f"),
                                                    sem("xn_f"), sem("xnT_f"))
        s_fh, s_fl, s_fh2, s_fl2 = sem("ffnT_hi_tile"), sem("ffnT_lo_tile"), sem("ffnT_hi"), sem("ffnT_lo")
        s_gz, s_nz, s_ez, s_rt, s_w, s_wT, s_wTs = (sem("gate_psum"), sem("neg_z"), sem("exp_neg_z"), sem("route_step"),
                                                    sem("weight"), sem("weightT_psum"), sem("weightT"))
        s_bdp, s_bds = sem("bd_psum"), sem("bd_term")
        s_u, s_ge, s_ah, s_al, s_y, s_ys, s_add, s_moeT, s_res = (
            sem("up"), sem("gelu"), sem("act_hi"), sem("act_lo"), sem("down"), sem("y_scaled"), sem("moe_add"),
            sem("moeT"), sem("result"))

        def wait(engine, semaphore, value):
            if not (isinstance(value, int) and value <= 0):
                engine.wait_ge(semaphore, value)

        def at(i, size):
            return bass.ds(i * size, size)

        def for_groups(engine, step, steps):
            for u in range(steps):
                step(0, u, True)
            with engine.Fori(1, NG - 1) as i:
                for u in range(steps):
                    step(i, u, True)
            for u in range(steps):
                step(NG - 1, u, False)

        block = ctx.enter_context(nc.Block())

        @block.sync
        def _(sp):
            xv = x_in.rearrange("b p d -> p b d")
            sp.dma_start(x[:, 0:GB, :], xv[:, 0:GB, :]).then_inc(s_x0, 16)
            sp.dma_start(ctxT[:, 0:TOK], ctxT_in[:, 0:TOK]).then_inc(s_x0, 16)
            sp.dma_start(mask8[:, :], mask_in).then_inc(s_mask, 16)
            sp.dma_start(wqkvo[:, :], wqkvo_in).then_inc(s_wa, 16)
            sp.dma_start(identf[:, :], ident_in).then_inc(s_small, 16)
            sp.dma_start(x[:, GB:NB, :], xv[:, GB:NB, :]).then_inc(s_xrest, 16)
            sp.dma_start(ctxT[:, TOK:NB * SEQ], ctxT_in[:, TOK:NB * SEQ]).then_inc(s_xrest, 16)
            sp.dma_start(gates[:, 0:1], g_x_in.partition_broadcast(128)).then_inc(s_small, 16)
            sp.dma_start(gates[:, 1:2], g_f_in.partition_broadcast(128)).then_inc(s_small, 16)
            sp.dma_start(earlier[:, :], earlier_in.partition_broadcast(128)).then_inc(s_small, 16)
            sp.dma_start(gate_b[:, :], gate_b_in.partition_broadcast(128)).then_inc(s_small, 16)
            sp.dma_start(gate_w[:, :], gate_wT_in).then_inc(s_small, 16)
            sp.dma_start(bu[:, :], bu_in).then_inc(s_small, 16)
            sp.dma_start(bd[:, :], bd_in).then_inc(s_small, 16)

            with sp.Fori(0, NG) as i:
                sp.wait_ge(s_ql, i + 1)
                sp.wait_ge(s_kl, i + 1)
                sp.dma_start(qk_dram[:, :, at(i, TOK)].rearrange("a r t -> r a t"),
                             arena[:, :, at(i, TOK)].bitcast(f32)).then_inc(s_qk_out, 16)

            def load_pair(i, h):
                first = i * TOK + h * 2 * SEQ
                for c in range(PARTS):
                    q_src = qk_dram[c // 2, :, bass.ds(first, 2 * SEQ)].rearrange("(g r) t -> r g t", g=UB)
                    sp.dma_start(q_pack[32 * c:32 * c + 32, h, :, :].bitcast(f32), q_src).then_inc(s_pack[h], 16)
                    for j in range(HU):
                        k_src = qk_dram[2 + c % 2, :, bass.ds(first, 2 * SEQ)].rearrange(
                            "(g j d) t -> j d g t", g=UB, j=HU)[j]
                        p = 32 * c + DH * j
                        sp.dma_start(k_pack[p:p + DH, h, :, j, :].bitcast(f32), k_src).then_inc(s_pack[h], 16)

            sp.wait_ge(s_pool0, 2)
            sp.wait_ge(s_qk_out, 16 * NG)
            for h in range(2):
                load_pair(0, h)
            with sp.Fori(1, NG) as i:
                for h in range(2):
                    sp.wait_ge(s_s, (i - 1) * UN + UN // 2 * (h + 1))
                    load_pair(i, h)

            def weights_round(j):
                sp.wait_ge(s_wTs, j + 1)
                sp.dma_start(w_dram[bass.ds(j, 1), :, :].rearrange("a e t -> (a e) t"),
                             weightT[1:E1, :]).then_inc(s_wt_out, 16)
                sp.wait_ge(s_wt_out, 16 * (j + 1))
                for e in range(E):
                    wait(sp, s_ys, E * (j - 1) + e + 1)
                    src = w_dram[bass.ds(j, 1), e, :].rearrange("a t -> (a t)").partition_broadcast(128)
                    sp.dma_start(weight_all[:, e, :], src).then_inc(s_wall, 16)

            weights_round(0)
            with sp.Fori(1, NG) as j:
                weights_round(j)
                sp.wait_ge(s_res, j)
                sp.dma_start(out_dram[at(j - 1, GB), :, :].rearrange("b p d -> p b d"), result[:, :, :]).then_inc(s_out, 16)
            sp.wait_ge(s_res, NG)
            sp.dma_start(out_dram[NB - GB:NB, :, :].rearrange("b p d -> p b d"), result[:, :, :]).then_inc(s_out, 16)
            sp.wait_ge(s_out, 16 * NG)

        @block.gpsimd
        def _(pool):
            g = nc.gpsimd
            g.memset(minus_half[:, :], -0.5).then_inc(s_pool0, 1)
            g.memset(k_pack[:, :, :, :, :].bitcast(f32), 0.0).then_inc(s_pool0, 1)
            g.memset(v_parts[:, :, :, VC - 1:VC], 1.0).then_inc(s_pool0, 1)
            g.memset(ones[:, :], 1.0).then_inc(s_pool0, 1)
            g.memset(e_const[:, :], float(np.e)).then_inc(s_pool0, 1)
            g.memset(weight[:, :, 0:1], SHARED_WEIGHT).then_inc(s_pool0, 1)
            pool.wait_ge(s_pool0, 6)
            pool.wait_ge(s_mk, 1)

            def stage_p(i):
                pool.wait_ge(s_ve, i + 1)
                g.tensor_tensor(inv_std[:, :], var_eps[:, :], minus_half[:, :], ALU.pow).then_inc(s_pw, 1)
                pool.wait_ge(s_pw, i + 1)
                g.tensor_tensor(inv_std_open[:, :], inv_std[:, :], row_open[:, 0:1].broadcast_to([128, GB]),
                                ALU.mult).then_inc(s_rs, 1)
                pool.wait_ge(s_ch, i + 1)
                g.tensor_tensor(cT_lo[:, :], ctxT[:, at(i, TOK)], cT_hi[:, :].bitcast(f32), ALU.subtract).then_inc(s_cl, 1)

            stage_p(0)
            with pool.Fori(1, NG) as i:
                stage_p(i)

            def load_w(i, k):
                g.dma_start(w_raw[:, k:k + 1, :], wffn_in[:, bass.ds(2 * i + k, 1), :]).then_inc(s_wraw[k], 16)

            def split_w(i, k):
                pool.wait_ge(s_wraw[k], 16 * (i + 1))
                hi, lo = w_hi[:, bass.ds(2 * i + k, 1), :], w_lo[:, bass.ds(2 * i + k, 1), :]
                g.tensor_tensor(hi, w_raw[:, k:k + 1, :], ones[:, :].rearrange("p (a n) -> p a n", a=1),
                                ALU.mult).then_inc(s_wh, 1)
                pool.wait_ge(s_wh, 2 * i + k + 1)
                g.tensor_tensor(lo, w_raw[:, k:k + 1, :], hi.bitcast(f32), ALU.subtract).then_inc(s_wl, 1)

            for k in range(2):
                load_w(0, k)
            with pool.Fori(0, E1 - 1) as i:
                for k in range(2):
                    split_w(i, k)
                    pool.wait_ge(s_wl, 2 * i + k + 1)
                    load_w(i + 1, k)
            for k in range(2):
                split_w(E1 - 1, k)

            def inverse_std(j):
                pool.wait_ge(s_ve2, j + 1)
                g.tensor_tensor(inv_std[:, :], var_eps[:, :], minus_half[:, :], ALU.pow).then_inc(s_rs2, 1)

            def exp_gate(j):
                pool.wait_ge(s_nz, j + 1)
                g.tensor_tensor(exp_neg_z[:, :, :], e_const[:, :].rearrange("p (t e) -> p t e", t=GB), neg_z[:, :, :],
                                ALU.pow).then_inc(s_ez, 1)

            def add(i, e):
                pool.wait_ge(s_ys, E * i + e)
                wait(pool, s_add, E * i + e - 1)
                if e == 1:
                    pool.wait_ge(s_bds, 2 * i + 2)
                g.tensor_tensor(moe[:, :], moe[:, :], y_scaled[:, e % 2, :], ALU.add).then_inc(s_add, 1)

            def stage_f(i, more):
                for e in range(1, E1):
                    add(i, e)
                    if more and e == 1:
                        inverse_std(i + 1)
                    if more and e == 3:
                        exp_gate(i + 1)

            inverse_std(0)
            exp_gate(0)
            stage_f(0, True)
            with pool.Fori(1, NG - 1) as i:
                stage_f(i, True)
            stage_f(NG - 1, False)

        @block.scalar
        def _(act_e):
            a = nc.scalar
            act_e.wait_ge(s_wa, 16)
            a.activation(wqkvo_hi[:, :], wqkvo[:, :], ACT.Copy).then_inc(s_wah, 1)

            def stage_p(i):
                if isinstance(i, int):
                    act_e.wait_ge(s_x0, 32)
                else:
                    act_e.wait_ge(s_xrest, 32)
                wait(act_e, s_v, i)
                wait(act_e, s_k, i)
                a.activation(cT_hi[:, :], ctxT[:, at(i, TOK)], ACT.Copy).then_inc(s_ch, 1)
                act_e.wait_ge(s_xT, i + 1)
                wait(act_e, s_q, i)
                a.activation(xnT_hi[:, :], bank[0][:, :], ACT.Copy).then_inc(s_xh, 1)
                act_e.wait_ge(s_k, i + 1)
                a.activation(arena[:, 2, at(i, TOK)], bank[2][:, :], ACT.Copy).then_inc(s_kh, 1)
                act_e.wait_ge(s_v, i + 1)
                a.activation(v_parts[:, at(i, GB), :, 0:DH],
                             bank[3][:, :].rearrange("p (b h d) -> p b h d", b=GB, h=HEADS), ACT.Copy).then_inc(s_vh, 1)
                act_e.wait_ge(s_q, i + 1)
                a.activation(arena[:, 0, at(i, TOK)], bank[1][:, :], ACT.Copy, scale=QSCALE).then_inc(s_qh, 1)

            stage_p(0)
            with act_e.Fori(1, NG) as i:
                stage_p(i)

            act_e.wait_ge(s_small, 16 * 8)
            a.activation(tanh_gates[:, :], gates[:, :], ACT.Tanh).then_inc(s_tanh, 1)
            a.activation(gate_hi[:, :], gate_w[:, :], ACT.Copy).then_inc(s_tanh, 1)

            def exps(n, u):
                act_e.wait_ge(s_mx, n + 1)
                wait(act_e, s_t, n - 1)
                for j in range(HU):
                    last = a.activation(prob[:, u % 2, j, :], bank[u % 4][:, SEQ * j:SEQ * (j + 1)], ACT.Exp,
                                        bias=neg_max[:, u % 4, j:j + 1])
                last.then_inc(s_ex, 1)

            def step(i, u, more):
                if u + 1 < UN or more:
                    exps(UN * i + u + 1, (u + 1) % UN)
                n = UN * i + u
                act_e.wait_ge(s_t, n + 1)
                wait(act_e, s_pv, n - 1)
                a.activation(probT_hi[:, u % 2, :], bank[4 + u % 2][:, :], ACT.Copy).then_inc(s_ph, 1)
                if u % UB == 1:
                    high_o(GB * i + u // UB - 1, (u // UB - 1) % 2)

            def high_o(b, par):
                if isinstance(b, int) and b < 0:
                    return
                act_e.wait_ge(s_oT, b + 1)
                wait(act_e, s_o, b - 1)
                a.activation(oT_hi[:, par, :], bank[6 + par][:, 0:SEQ], ACT.Copy).then_inc(s_oh, 1)

            exps(0, 0)
            for_groups(act_e, step, UN)
            high_o(NB - 1, 1)

            def tile_high(j):
                act_e.wait_ge(s_xT2, j + 1)
                wait(act_e, s_gz, j)
                a.activation(xnT_hi[:, :], bank[6][:, :], ACT.Copy).then_inc(s_fh, 1)

            def keep_parts(j):
                act_e.wait_ge(s_fh, j + 1)
                a.activation(ffnT_hi[:, at(j, TOK)], xnT_hi[:, :].bitcast(f32), ACT.Copy).then_inc(s_fh2, 1)
                act_e.wait_ge(s_fl, j + 1)
                a.activation(ffnT_lo[:, at(j, TOK)], xnT_lo[:, :].bitcast(f32), ACT.Copy).then_inc(s_fl2, 1)

            def weight_rows(j):
                act_e.wait_ge(s_wT, j + 1)
                wait(act_e, s_wt_out, 16 * j)
                wait(act_e, s_bdp, j)
                a.activation(weightT[:, :], bank[7][0:E1, :], ACT.Copy).then_inc(s_wTs, 1)

            def bias_term(i):
                act_e.wait_ge(s_bdp, i + 1)
                wait(act_e, s_moeT, i)
                a.activation(moe[:, :], bank[6][:, :], ACT.Copy).then_inc(s_bds, 1)

            def ffn_step(i, n, more):
                m = CH * i + n
                act_e.wait_ge(s_u, m + 1)
                wait(act_e, s_al, m - 3)
                a.activation(act[:, n % 4, :], bank[n % 4][:, :], ACT.Gelu, bias=bu[:, n:n + 1]).then_inc(s_ge, 1)
                if n:
                    high_act(m - 1, n - 1)
                if n == CH - 1:
                    high_act(m, n)
                if n == 4:
                    bias_term(i)
                if more and n == 13:
                    tile_high(i + 1)
                if more and n == 18:
                    keep_parts(i + 1)
                if more and n == 28:
                    weight_rows(i + 1)

            def high_act(m, n):
                act_e.wait_ge(s_ge, m + 1)
                wait(act_e, s_down_of(m), m - 3)
                a.activation(act_hi[:, n % 4, :], act[:, n % 4, :], ACT.Copy).then_inc(s_ah, 1)

            def s_down_of(m):
                return s_y

            act_e.wait_ge(s_ol, NB)
            tile_high(0)
            keep_parts(0)
            weight_rows(0)
            for_groups(act_e, ffn_step, CH)

        @block.vector
        def _(dve):
            v = nc.vector
            dve.wait_ge(s_mask, 16)
            v.tensor_copy(maskf[:, :], mask8[:, :]).then_inc(s_ib, 1)
            dve.wait_ge(s_ib, 1)
            v.reduce_max(row_open[:, :], maskf[:, :], AX.X).then_inc(s_mk, 1)
            v.tensor_scalar(mask_low[:, :], maskf[:, :], 1.0, MASKED, ALU.subtract, ALU.mult).then_inc(s_ib, 1)
            dve.wait_ge(s_mk, 1)
            dve.wait_ge(s_ib, 2)
            v.tensor_scalar(mask_bias[:, :], mask_low[:, :], row_open[:, 0:1], None, ALU.mult).then_inc(s_mk, 1)

            def norm_stats(i, smv, sve):
                for t in range(GB):
                    v.bn_stats(stats[:, t, :], x[:, at(i * GB + t, 1), :].rearrange("p a d -> p (a d)"))
                dve.drain()
                for t in range(GB):
                    v.bn_aggr(mean_var[:, t, :], stats[:, t, :]).then_inc(smv, 1)
                dve.wait_ge(smv, GB * i + GB)
                v.tensor_scalar(var_eps[:, :], mean_var[:, :, 1], EPS, None, ALU.add).then_inc(sve, 1)

            def norm_apply(i, scale, sxn):
                for t in range(GB):
                    v.tensor_scalar(xn[:, t, :], x[:, at(i * GB + t, 1), :].rearrange("p a d -> p (a d)"),
                                    mean_var[:, t, 0:1], scale[:, t:t + 1], ALU.subtract, ALU.mult).then_inc(sxn, 1)

            def stage_p(i):
                if isinstance(i, int):
                    dve.wait_ge(s_x0, 32)
                else:
                    dve.wait_ge(s_xrest, 32)
                norm_stats(i, s_mv, s_ve)
                dve.wait_ge(s_rs, i + 1)
                wait(dve, s_xT, i)
                norm_apply(i, inv_std_open, s_xn)
                dve.wait_ge(s_xh, i + 1)
                v.tensor_tensor(xnT_lo[:, :], bank[0][:, :], xnT_hi[:, :].bitcast(f32), ALU.subtract).then_inc(s_xl, 1)
                dve.wait_ge(s_kh, i + 1)
                v.tensor_tensor(arena[:, 3, at(i, TOK)], bank[2][:, :], arena[:, 2, at(i, TOK)].bitcast(f32),
                                ALU.subtract).then_inc(s_kl, 1)
                dve.wait_ge(s_vh, i + 1)
                wait(dve, s_vl, i)
                v.tensor_tensor(v_rest[:, :, :, :].rearrange("p b h d -> p (b h) d"),
                                bank[3][:, :].rearrange("p (n d) -> p n d", d=DH),
                                v_parts[:, at(i, GB), :, 0:DH].rearrange("p b h d -> p (b h) d"),
                                ALU.subtract).then_inc(s_vr, 1)
                dve.wait_ge(s_qh, i + 1)
                v.scalar_tensor_tensor(arena[:, 1, at(i, TOK)], bank[1][:, :], QSCALE,
                                       arena[:, 0, at(i, TOK)].bitcast(f32), ALU.mult, ALU.subtract).then_inc(s_ql, 1)
                dve.wait_ge(s_vr, i + 1)
                v.tensor_copy(v_parts[:, at(i, GB), :, DH:2 * DH].rearrange("p b h d -> p (b h) d"),
                              v_rest[:, :, :, :].rearrange("p b h d -> p (b h) d")).then_inc(s_vm, 1)
                dve.wait_ge(s_vm, i + 1)
                v.tensor_tensor(v_parts[:, at(i, GB), :, 2 * DH:3 * DH].rearrange("p b h d -> p (b h) d"),
                                v_rest[:, :, :, :].rearrange("p b h d -> p (b h) d"),
                                v_parts[:, at(i, GB), :, DH:2 * DH].rearrange("p b h d -> p (b h) d"),
                                ALU.subtract).then_inc(s_vl, 1)

            dve.wait_ge(s_small, 16 * 8)
            v.tensor_copy(identb[:, :], identf[:, :]).then_inc(s_ib, 1)
            dve.wait_ge(s_wah, 1)
            v.tensor_tensor(wqkvo_lo[:, :], wqkvo[:, :], wqkvo_hi[:, :].bitcast(f32), ALU.subtract).then_inc(s_wal, 1)
            stage_p(0)
            with dve.Fori(1, NG) as i:
                stage_p(i)
            dve.wait_ge(s_tanh, 2)
            v.tensor_tensor(gate_lo[:, :], gate_w[:, :], gate_hi[:, :].bitcast(f32), ALU.subtract).then_inc(s_wal, 1)

            def maxima(n, u):
                dve.wait_ge(s_s, n + 1)
                v.tensor_reduce(neg_max[:, u % 4, :], bank[u % 4][:, :].rearrange("p (j k) -> p j k", j=HU), AX.X,
                                ALU.max, negate=True).then_inc(s_mx, 1)

            def normalize(b, par):
                if isinstance(b, int) and b < 0:
                    return
                dve.wait_ge(s_pv, UB * b + UB)
                o = bank[6 + par][:, 0:HEADS * VC].rearrange("p (h c) -> p h c", c=VC)
                v.tensor_reduce(o_sum[:, :, :], o[:, :, 0:3 * DH].rearrange("p h (c d) -> p h d c", c=3), AX.X,
                                ALU.add).then_inc(s_os, 1)
                v.reciprocal(inv_sum[:, :], o[:, :, VC - 1]).then_inc(s_os, 1)
                dve.wait_ge(s_os, 2 * b + 2)
                v.tensor_tensor(o_norm[:, par, :, :], o_sum[:, :, :],
                                inv_sum[:, :].rearrange("p (h a) -> p h a", a=1).broadcast_to([128, HEADS, DH]),
                                ALU.mult).then_inc(s_on, 1)

            def low_o(b, par):
                if isinstance(b, int) and b < 0:
                    return
                dve.wait_ge(s_oh, b + 1)
                v.tensor_tensor(oT_lo[:, par, :], bank[6 + par][:, 0:SEQ], oT_hi[:, par, :].bitcast(f32),
                                ALU.subtract).then_inc(s_ol, 1)

            def residual(b, par):
                if isinstance(b, int) and b < 0:
                    return
                dve.wait_ge(s_o, b + 1)
                xb = x[:, at(b, 1), :].rearrange("p a d -> p (a d)")
                v.scalar_tensor_tensor(xb, bank[6 + par][:, SEQ:SEQ + D], tanh_gates[:, 0:1], xb, ALU.mult,
                                       ALU.add).then_inc(s_x2, 1)

            def step(i, u, more):
                if u + 2 < UN or more:
                    maxima(UN * i + u + 2, (u + 2) % UN)
                n = UN * i + u
                dve.wait_ge(s_ph, n + 1)
                v.tensor_tensor(probT_lo[:, u % 2, :], bank[4 + u % 2][:, :], probT_hi[:, u % 2, :],
                                ALU.subtract).then_inc(s_pl, 1)
                b, par = GB * i + u // UB - 1, (u // UB - 1) % 2
                if u % UB == 0:
                    normalize(b, par)
                if u % UB == 1:
                    low_o(b, par)
                if u % UB == 2:
                    residual(b, par)

            maxima(0, 0)
            maxima(1, 1)
            for_groups(dve, step, UN)
            normalize(NB - 1, 1)
            low_o(NB - 1, 1)
            residual(NB - 1, 1)

            def xn_parts(j):
                dve.wait_ge(s_fh, j + 1)
                v.tensor_tensor(xnT_lo[:, :], bank[6][:, :], xnT_hi[:, :].bitcast(f32), ALU.subtract).then_inc(s_fl, 1)

            def gate_logits(j):
                dve.wait_ge(s_gz, j + 1)
                v.scalar_tensor_tensor(neg_z[:, :, :], bank[7][:, 0:GB * E].rearrange("p (t e) -> p t e", t=GB), -1.0,
                                       gate_b[:, :].rearrange("p (a e) -> p a e", a=1).broadcast_to([128, GB, E]),
                                       ALU.mult, ALU.subtract).then_inc(s_nz, 1)

            def route(j):
                steps = 9
                dve.wait_ge(s_ez, j + 1)
                v.tensor_scalar(sig_den[:, :, :], exp_neg_z[:, :, :], 1.0, None, ALU.add).then_inc(s_rt, 1)
                dve.wait_ge(s_rt, steps * j + 1)
                v.reciprocal(sig[:, :, :], sig_den[:, :, :]).then_inc(s_rt, 1)
                dve.wait_ge(s_rt, steps * j + 2)
                this = sig[:, :, :].rearrange("p t (e a) -> p t e a", a=1).broadcast_to([128, GB, E, E])
                other = sig[:, :, :].rearrange("p t (a e) -> p t a e", a=1).broadcast_to([128, GB, E, E])
                v.tensor_tensor(beats[:, :, :, :], other, this, ALU.is_gt).then_inc(s_rt, 1)
                v.tensor_tensor(ties[:, :, :, :], other, this, ALU.is_equal).then_inc(s_rt, 1)
                dve.wait_ge(s_rt, steps * j + 4)
                flat = ties[:, :, :, :].rearrange("p t e f -> p t (e f)")
                before = earlier[:, :].rearrange("p (a n) -> p a n", a=1).broadcast_to([128, GB, E * E])
                v.tensor_tensor(flat, flat, before, ALU.mult).then_inc(s_rt, 1)
                dve.wait_ge(s_rt, steps * j + 5)
                v.tensor_tensor(beats[:, :, :, :], beats[:, :, :, :], ties[:, :, :, :], ALU.add).then_inc(s_rt, 1)
                dve.wait_ge(s_rt, steps * j + 6)
                v.tensor_reduce(rank[:, :, :], beats[:, :, :, :], AX.X, ALU.add).then_inc(s_rt, 1)
                dve.wait_ge(s_rt, steps * j + 7)
                v.scalar_tensor_tensor(sig_top[:, :, :], rank[:, :, :], 2.0, sig[:, :, :], ALU.is_lt,
                                       ALU.mult).then_inc(s_rt, 1)
                dve.wait_ge(s_rt, steps * j + 8)
                v.tensor_reduce(top_sum[:, :], sig_top[:, :, :], AX.X, ALU.add).then_inc(s_rt, 1)
                dve.wait_ge(s_rt, steps * j + 9)
                v.tensor_scalar(top_sum[:, :], top_sum[:, :], TINY, None, ALU.add).then_inc(s_w, 1)
                dve.wait_ge(s_w, 3 * j + 1)
                v.reciprocal(inv_top[:, :], top_sum[:, :]).then_inc(s_w, 1)
                dve.wait_ge(s_w, 3 * j + 2)
                wait(dve, s_wT, j)
                v.tensor_tensor(weight[:, :, 1:E1], sig_top[:, :, :],
                                inv_top[:, :].rearrange("p (t a) -> p t a", a=1).broadcast_to([128, GB, E]),
                                ALU.mult).then_inc(s_w, 1)

            def combine(i, e):
                dve.wait_ge(s_y, CH * i + FC * e + FC)
                y = bank[4 + e % 2]
                if e == 0:
                    dve.wait_ge(s_bds, 2 * i + 1)
                    v.scalar_tensor_tensor(moe[:, :], y[:, :], SHARED_WEIGHT, moe[:, :], ALU.mult,
                                           ALU.add).then_inc(s_bds, 1)
                else:
                    dve.wait_ge(s_wall, 16 * (E * i + E))
                    wait(dve, s_add, E * i + e - 2)
                    v.tensor_tensor(y_scaled[:, e % 2, :], y[:, :], weight_all[:, e - 1, :], ALU.mult).then_inc(s_ys, 1)

            def finish(i):
                if isinstance(i, int) and i < 0:
                    return
                dve.wait_ge(s_moeT, i + 1)
                wait(dve, s_out, 16 * i)
                v.scalar_tensor_tensor(result[:, :, :], bank[7][:, :].rearrange("p (b d) -> p b d", b=GB),
                                       tanh_gates[:, 1:2], x[:, at(i, GB), :], ALU.mult, ALU.add).then_inc(s_res, 1)

            def ffn_step(i, n, more):
                m = CH * i + n
                dve.wait_ge(s_ah, m + 1)
                wait(dve, s_y, m - 3)
                v.tensor_tensor(act_lo[:, n % 4, :], act[:, n % 4, :], act_hi[:, n % 4, :].bitcast(f32),
                                ALU.subtract).then_inc(s_al, 1)
                if n % FC == 1 and n > FC:
                    combine(i, n // FC - 1)
                if n == 3:
                    finish(i - 1)
                if n == CH - 1:
                    combine(i, E)
                if more and n == 6:
                    norm_stats(i + 1, s_mv2, s_ve2)
                if more and n == 10:
                    dve.wait_ge(s_rs2, i + 2)
                    norm_apply(i + 1, inv_std, s_xn2)
                if more and n == 14:
                    xn_parts(i + 1)
                if more and n == 18:
                    gate_logits(i + 1)
                if more and n == 22:
                    route(i + 1)

            dve.wait_ge(s_x2, NB)
            norm_stats(0, s_mv2, s_ve2)
            dve.wait_ge(s_rs2, 1)
            norm_apply(0, inv_std, s_xn2)
            xn_parts(0)
            gate_logits(0)
            route(0)
            for_groups(dve, ffn_step, CH)
            finish(NG - 1)

        @block.tensor
        def _(pe):
            mm = nc.tensor.matmul

            def three(out, w_h, w_l, r_h, r_l, start=True, stop=True):
                mm(out, w_h, r_h, start=start, stop=False)
                mm(out, w_l, r_h, start=False, stop=False)
                return mm(out, w_h, r_l, start=False, stop=stop)

            def wa(part, k):
                return part[:, D * k:D * (k + 1)]

            pe.wait_ge(s_small, 16 * 8)
            pe.wait_ge(s_wah, 1)
            pe.wait_ge(s_wal, 1)

            def stage_p(i):
                pe.wait_ge(s_cl, i + 1)
                wait(pe, s_kl, i)
                three(bank[2][:, :], wa(wqkvo_hi, 1), wa(wqkvo_lo, 1), cT_hi[:, :], cT_lo[:, :]).then_inc(s_k, 1)
                pe.wait_ge(s_xn, GB * i + GB)
                wait(pe, s_xl, i)
                for t in range(GB):
                    last = nc.tensor.transpose(bank[0][:, D * t:D * (t + 1)], xn[:, t, :], identf[:, :])
                last.then_inc(s_xT, 1)
                wait(pe, s_vr, i)
                for t in range(GB):
                    c = slice(SEQ * t, SEQ * (t + 1))
                    last = three(bank[3][:, c], cT_hi[:, c], cT_lo[:, c], wa(wqkvo_hi, 2), wa(wqkvo_lo, 2))
                last.then_inc(s_v, 1)
                pe.wait_ge(s_xl, i + 1)
                wait(pe, s_ql, i)
                three(bank[1][:, :], wa(wqkvo_hi, 0), wa(wqkvo_lo, 0), xnT_hi[:, :], xnT_lo[:, :]).then_inc(s_q, 1)

            stage_p(0)
            with pe.Fori(1, NG) as i:
                stage_p(i)

            def scores(i, u):
                b, g = u // UB, u % UB
                h = b // 2
                if u % (UN // 2) == 0:
                    pe.wait_ge(s_pack[h], 16 * PARTS * (1 + HU) * (i + 1))
                out = bank[u % 4]
                t = slice(SEQ * (b % 2), SEQ * (b % 2 + 1))
                out4 = out[:, :].rearrange("p (j k) -> p j k", j=HU)
                mm(out4, q_pack[:, h, g, t], k_pack[:, h, g, :, t], start=True, stop=False)
                mm(out4, identb[:, :],
                   mask_bias[:, :].rearrange("p (a k) -> p a k", a=1).broadcast_to([128, HU, SEQ]),
                   start=False, stop=True).then_inc(s_s, 1)

            def pv(i, u):
                b, g = u // UB, u % UB
                n = UN * i + u
                pe.wait_ge(s_pl, n + 1)
                if g == 0:
                    wait(pe, s_x2, GB * i + b - 1)
                for j in range(HU):
                    h = HU * g + j
                    out = bank[6 + b % 2][:, VC * h:VC * (h + 1)]
                    rhs = v_parts[:, at(GB * i + b, 1), h, :].rearrange("p a c -> p (a c)")
                    mm(out, probT_hi[:, u % 2, SEQ * j:SEQ * (j + 1)], rhs, start=True, stop=False)
                    last = mm(out, probT_lo[:, u % 2, SEQ * j:SEQ * (j + 1)], rhs, start=False, stop=True)
                last.then_inc(s_pv, 1)

            def o_transpose(b, par):
                if isinstance(b, int) and b < 0:
                    return
                pe.wait_ge(s_on, b + 1)
                nc.tensor.transpose(bank[6 + par][:, 0:SEQ], o_norm[:, par, :, :].rearrange("p h d -> p (h d)"),
                                    identf[:, :]).then_inc(s_oT, 1)

            def wo(b, par):
                if isinstance(b, int) and b < 0:
                    return
                pe.wait_ge(s_ol, b + 1)
                three(bank[6 + par][:, SEQ:SEQ + D], oT_hi[:, par, :], oT_lo[:, par, :], wa(wqkvo_hi, 3),
                      wa(wqkvo_lo, 3)).then_inc(s_o, 1)

            def step(i, u, more):
                n = UN * i + u
                wait(pe, s_ex, n)
                if u + 3 < UN:
                    scores(i, u + 3)
                elif more:
                    scores(i + 1, u + 3 - UN)
                pe.wait_ge(s_ex, n + 1)
                wait(pe, s_pl, n - 1)
                for j in range(HU):
                    last = nc.tensor.transpose(bank[4 + u % 2][:, SEQ * j:SEQ * (j + 1)], prob[:, u % 2, j, :],
                                               identf[:, :])
                last.then_inc(s_t, 1)
                b, par = GB * i + u // UB - 1, (u // UB - 1) % 2
                if u % UB == 1:
                    o_transpose(b, par)
                if u % UB == 2:
                    wo(b, par)
                if u:
                    pv(i, u - 1)
                elif not (isinstance(i, int) and i == 0):
                    pv(i - 1, UN - 1)

            pe.wait_ge(s_mk, 2)
            pe.wait_ge(s_ib, 3)
            pe.wait_ge(s_xl, NG)
            pe.wait_ge(s_kl, NG)
            pe.wait_ge(s_vr, NG)
            pe.wait_ge(s_ql, NG)
            pe.wait_ge(s_vl, NG)
            pe.wait_ge(s_pool0, 6)
            for u in range(3):
                scores(0, u)
            for_groups(pe, step, UN)
            pv(NG - 1, UN - 1)
            o_transpose(NB - 1, 1)
            wo(NB - 1, 1)

            def ffn_transpose(j):
                pe.wait_ge(s_xn2, GB * j + GB)
                wait(pe, s_bds, 2 * j)
                for t in range(GB):
                    last = nc.tensor.transpose(bank[6][:, D * t:D * (t + 1)], xn[:, t, :], identf[:, :])
                last.then_inc(s_xT2, 1)

            def gate(j):
                pe.wait_ge(s_fl, j + 1)
                wait(pe, s_res, j - 1)
                for t in range(GB):
                    c = slice(SEQ * t, SEQ * (t + 1))
                    last = three(bank[7][:, E * t:E * (t + 1)], xnT_hi[:, c], xnT_lo[:, c], gate_hi[:, :], gate_lo[:, :])
                last.then_inc(s_gz, 1)

            def weight_transpose(j):
                pe.wait_ge(s_w, 3 * j + 3)
                for t in range(GB):
                    last = nc.tensor.transpose(bank[7][0:E1, SEQ * t:SEQ * (t + 1)], weight[:, t, :], identf[:, :])
                last.then_inc(s_wT, 1)

            def bias_term(i):
                pe.wait_ge(s_wTs, i + 1)
                pe.wait_ge(s_fh2, i + 1)
                mm(bank[6][:, :], bd[:, :], weightT[:, :], start=True, stop=True).then_inc(s_bdp, 1)

            def up(i, n):
                m = CH * i + n
                e, c = n // FC, n % FC
                wait(pe, s_ge, m - 3)
                if n == 0:
                    pe.wait_ge(s_fl2, i + 1)
                k = slice(D * c, D * (c + 1))
                three(bank[n % 4][:, :], w_hi[:, e, k], w_lo[:, e, k], ffnT_hi[:, at(i, TOK)],
                      ffnT_lo[:, at(i, TOK)]).then_inc(s_u, 1)

            def down(i, n):
                m = CH * i + n
                e, c = n // FC, n % FC
                pe.wait_ge(s_al, m + 1)
                if c == 0:
                    wait(pe, s_ys, E * i + e - 2 if e else E * i)
                    if e == 2:
                        pe.wait_ge(s_bds, 2 * i + 2)
                k = slice(D * c, D * (c + 1))
                three(bank[4 + e % 2][:, :], w_hi[:, E1 + e, k], w_lo[:, E1 + e, k], act_hi[:, n % 4, :],
                      act_lo[:, n % 4, :], start=(c == 0), stop=(c == FC - 1)).then_inc(s_y, 1)

            def moe_transpose(i):
                if isinstance(i, int) and i < 0:
                    return
                pe.wait_ge(s_add, E * i + E)
                pe.wait_ge(s_wTs, min(NG, i + 2) if isinstance(i, int) else i + 2)
                for t in range(GB):
                    last = nc.tensor.transpose(bank[7][:, D * t:D * (t + 1)], moe[:, SEQ * t:SEQ * (t + 1)], identf[:, :])
                last.then_inc(s_moeT, 1)

            def ffn_step(i, n, more):
                if n + 3 < CH:
                    up(i, n + 3)
                elif more:
                    up(i + 1, n + 3 - CH)
                down(i, n)
                if n == 1:
                    moe_transpose(i - 1)
                if more and n == 12:
                    ffn_transpose(i + 1)
                if more and n == 16:
                    gate(i + 1)
                if more and n == 25:
                    weight_transpose(i + 1)
                if n == 0:
                    bias_term(i)

            pe.wait_ge(s_wal, 2)
            pe.wait_ge(s_x2, NB)
            ffn_transpose(0)
            gate(0)
            weight_transpose(0)
            pe.wait_ge(s_wl, 2 * E1)
            for n in range(3):
                up(0, n)
            for_groups(pe, ffn_step, CH)
            moe_transpose(NG - 1)


def kernel(x, ctx_1024, mask_SxS2_bk0, g_xattn, g_ffn, L0_xattn_Wq, L0_xattn_Wk, L0_xattn_Wv, L0_xattn_Wo,
           L0_ffn_gate_w, L0_ffn_gate_bias, L0_ffn_Wu, L0_ffn_bu, L0_ffn_Wd, L0_ffn_bd, L0_ffn_sWu, L0_ffn_sbu,
           L0_ffn_sWd, L0_ffn_sbd):
    import concourse.bacc as bacc
    from concourse.bass_utils import run_bass_kernel_spmd

    def host(a):
        return np.ascontiguousarray(np.asarray(a))

    x = host(x)
    NB, SEQ, D = x.shape
    E, F = host(L0_ffn_bu).shape
    ctxT = host(host(ctx_1024).reshape(NB * SEQ, D).T)
    wqkvo = host(np.stack([host(w).T for w in (L0_xattn_Wq, L0_xattn_Wk, L0_xattn_Wv, L0_xattn_Wo)], 1).reshape(D, 4 * D))
    wu = np.concatenate([host(L0_ffn_sWu)[None], host(L0_ffn_Wu)], 0)
    wd = np.concatenate([host(L0_ffn_sWd)[None], host(L0_ffn_Wd)], 0)
    up = wu.transpose(2, 0, 1)
    down = wd.reshape(E + 1, D, F // 128, 128).transpose(3, 0, 2, 1).reshape(128, E + 1, F)
    wffn = host(np.concatenate([up, down], 1))
    bu = host(np.concatenate([host(L0_ffn_sbu)[None], host(L0_ffn_bu)], 0).reshape(-1, 128).T)
    bd = host(np.concatenate([host(L0_ffn_sbd)[None], host(L0_ffn_bd)], 0))
    arrays = {
        "x_in": x, "ctxT_in": ctxT, "mask_in": host(mask_SxS2_bk0), "g_x_in": host(g_xattn),
        "g_f_in": host(g_ffn), "wqkvo_in": wqkvo, "wffn_in": wffn, "bu_in": bu, "bd_in": bd,
        "gate_wT_in": host(host(L0_ffn_gate_w).T), "gate_b_in": host(L0_ffn_gate_bias),
        "ident_in": np.eye(128, dtype=np.float32),
        "earlier_in": np.tril(np.ones((E, E), np.float32), -1).reshape(-1),
    }
    nc = bacc.Bacc("TRN2", target_bir_lowering=False, num_devices=1)
    args = [nc.dram_tensor(n, a.shape, mybir.dt.from_np(a.dtype), kind="ExternalInput").ap() for n, a in arrays.items()]
    out = nc.dram_tensor("out", (NB, SEQ, D), mybir.dt.float32, kind="ExternalOutput").ap()
    build(nc, *args, out)
    r = run_bass_kernel_spmd(nc, [arrays], core_ids=[0])
    return r.results[0]["out"]
```

```python
from contextlib import ExitStack

import concourse.bass as bass
import concourse.mybir as mybir
import numpy as np


def build(nc, x_in, ctxT_in, mask_in, g_x_in, g_f_in, wqkvo_in, wffn_in, bu_in, bd_in, gate_wT_in, gate_b_in,
          ident_in, earlier_in, out_dram):
    f32, f32r, bf16, fp16, u8 = (mybir.dt.float32, mybir.dt.float32r, mybir.dt.bfloat16, mybir.dt.float16,
                                 mybir.dt.uint8)
    ALU, ACT, AX = mybir.AluOpType, mybir.ActivationFunctionType, mybir.AxisListType

    NB, SEQ, D = x_in.shape
    HEADS, DH = 16, D // 16
    E1 = wffn_in.shape[1] // 2
    E = E1 - 1
    GB = 4
    NG = NB // GB
    TOK = GB * SEQ
    HU = 4
    UB = HEADS // HU
    UN = GB * UB
    PARTS = ((0, 0), (1, 0), (0, 1))
    KR = len(PARTS) * HU * DH
    VC = 3 * DH + 1
    FC = wffn_in.shape[2] // D
    CH = E1 * FC
    EPS, MASKED, TINY = 1e-5, 1e9, 1e-6
    QSCALE = float(1.0 / np.sqrt(np.float32(DH)))
    SHARED_WEIGHT = 0.1

    qk_dram = nc.dram_tensor("qk_dram", (4, D, NB * SEQ), f32, kind="Internal").ap()
    w_dram = nc.dram_tensor("w_dram", (NG, E, TOK), f32, kind="Internal").ap()

    ctx = ExitStack()
    with ctx:
        def sb(name, shape, dt):
            return ctx.enter_context(nc.sbuf_tensor(name, shape, dt))

        def sem(name):
            return ctx.enter_context(nc.semaphore(name))

        bank = [ctx.enter_context(nc.psum_tensor(f"bank{i}", [128, 512], f32)) for i in range(8)]

        identf = sb("identf", [128, 128], f32)
        identb = sb("identb", [128, 128], bf16)
        earlier = sb("earlier", [128, E * E], f32)
        ones = sb("ones", [128, 512], f32)
        minus_half = sb("minus_half", [128, GB], f32)
        e_const = sb("e_const", [128, GB * E], f32)
        mask8 = sb("mask8", [128, SEQ], u8)
        mask_bias = sb("mask_bias", [128, SEQ], bf16)
        row_open = sb("row_open", [128, 1], f32)
        gates = sb("gates", [128, 2], f32)
        tanh_gates = sb("tanh_gates", [128, 2], f32)
        wqkvo = sb("wqkvo", [128, 4 * D], f32)
        wqkvo_hi = sb("wqkvo_hi", [128, 4 * D], f32r)
        wqkvo_lo = sb("wqkvo_lo", [128, 4 * D], f32r)
        gate_w = sb("gate_w", [128, E], f32)
        gate_hi = sb("gate_hi", [128, E], f32r)
        gate_lo = sb("gate_lo", [128, E], f32r)
        gate_b = sb("gate_b", [128, E], f32)
        bu = sb("bu", [128, CH], f32)
        bd = sb("bd", [E1, D], f32)
        w_raw = sb("w_raw", [128, 2, 512], f32)
        w_hi = sb("w_hi", [128, 2 * E1, 512], f32r)
        w_lo = sb("w_lo", [128, 2 * E1, 512], f32r)

        x = sb("x", [128, NB, D], f32)
        ctxT = sb("ctxT", [128, NB * SEQ], f32)
        stats = sb("stats", [128, GB, 6], f32)
        mean_var = sb("mean_var", [128, GB, 2], f32)
        var_eps = sb("var_eps", [128, GB], f32)
        inv_std = sb("inv_std", [128, GB], f32)
        inv_std_open = sb("inv_std_open", [128, GB], f32)
        xn = sb("xn", [128, GB, D], f32)
        xnT_hi = sb("xnT_hi", [128, TOK], f32r)
        xnT_lo = sb("xnT_lo", [128, TOK], f32r)
        arena = sb("arena", [128, 4, 4 * TOK], f32r)
        q_hi, q_lo, k_hi, k_lo = (arena[:, a, 0:TOK] for a in range(4))
        k_parts = arena[:, 2:4, 0:TOK]
        cT_hi, cT_lo = arena[:, 0, TOK:2 * TOK], arena[:, 1, TOK:2 * TOK]
        act_hi = arena[:, 0, :].rearrange("p (s n) -> p s n", s=4)
        act_lo = arena[:, 1, :].rearrange("p (s n) -> p s n", s=4)
        ffnT_hi, ffnT_lo = arena[:, 2, :], arena[:, 3, :]
        v_parts = sb("v_parts", [128, NB, HEADS, VC], bf16)
        q_pack = sb("q_pack", [KR, 2, UB, 2 * SEQ], f32r)
        k_pack = sb("k_pack", [128, 2, UB, HU, 2 * SEQ], f32r)
        neg_max = sb("neg_max", [128, 4, HU], f32)
        weight_all = k_pack[:, 0, :, :, :].rearrange("p g j k -> p (g j k)").bitcast(f32).rearrange(
            "p (e t) -> p e t", e=E)
        prob = sb("prob", [128, 2, HU, SEQ], f32)
        maskf, mask_low = prob[:, 0, 0, :], prob[:, 0, 1, :]
        v_rest = wqkvo[:, :].rearrange("p (b h d) -> p b h d", b=GB, h=HEADS)
        y_scaled = prob[:, :, :, :].rearrange("p a b c -> p a (b c)")
        probT_hi = sb("probT_hi", [128, 2, HU * SEQ], fp16)
        probT_lo = sb("probT_lo", [128, 2, HU * SEQ], fp16)
        bias_sum = probT_hi[:, :, :].rearrange("p a n -> p (a n)").bitcast(f32)
        o_sum = sb("o_sum", [128, HEADS, DH], f32)
        inv_sum = sb("inv_sum", [128, HEADS], f32)
        o_norm = sb("o_norm", [128, 2, HEADS, DH], f32)
        oT_hi = sb("oT_hi", [128, 2, SEQ], f32r)
        oT_lo = sb("oT_lo", [128, 2, SEQ], f32r)
        neg_z = sb("neg_z", [128, GB, E], f32)
        exp_neg_z = sb("exp_neg_z", [128, GB, E], f32)
        sig_den = sb("sig_den", [128, GB, E], f32)
        sig = sb("sig", [128, GB, E], f32)
        compare = wqkvo[:, :].rearrange("p (a t e f) -> p a t e f", a=2, t=GB, e=E)
        beats, ties = compare[:, 0], compare[:, 1]
        rank = sb("rank", [128, GB, E], f32)
        sig_top = sb("sig_top", [128, GB, E], f32)
        top_sum = sb("top_sum", [128, GB], f32)
        inv_top = sb("inv_top", [128, GB], f32)
        weight = sb("weight", [128, GB, E1], f32)
        weightT = sb("weightT", [E1, TOK], f32)
        act = ctxT[:, :].rearrange("p (s n) -> p s n", s=4)
        moe = w_raw[:, 1, :]
        result = w_raw[:, 0, :].rearrange("p (b d) -> p b d", b=GB)

        s_mask, s_ident, s_small, s_wa, s_x0, s_xrest = sem("mask_in"), sem("ident_in"), sem("small_in"), sem("wa_in"), sem("x0_in"), sem("xrest_in")
        s_wraw = [sem("wraw_even"), sem("wraw_odd")]
        s_k_out, s_q_out = sem("k_out"), sem("q_out")
        s_qpack = [sem("q_pack_even"), sem("q_pack_odd")]
        s_kpack = [sem("k_pack_even"), sem("k_pack_odd")]
        s_wt_out, s_wall, s_out = sem("weightT_out"), sem("weight_all_in"), sem("out")
        s_pool0, s_mk, s_wah, s_wal, s_tanh, s_ib = (sem("pool_constants"), sem("mask_done"), sem("wa_hi"), sem("wa_lo"),
                                                    sem("tanh_done"), sem("identb_done"))
        s_wh, s_wl = sem("ffn_w_hi"), sem("ffn_w_lo")
        s_mv, s_ve, s_pw, s_rs = sem("mean_var_p"), sem("var_eps_p"), sem("pow_p"), sem("inv_std_p")
        s_xn, s_xT, s_xh, s_xl = sem("xn_p"), sem("xnT_psum"), sem("xnT_hi"), sem("xnT_lo")
        s_ch, s_cl, s_q, s_k, s_v = sem("cT_hi"), sem("cT_lo"), sem("q_psum"), sem("k_psum"), sem("v_psum")
        s_qh, s_ql, s_kh, s_kl = sem("q_hi"), sem("q_lo"), sem("k_hi"), sem("k_lo")
        s_vh, s_vr, s_vm, s_vl = sem("v_high"), sem("v_rest"), sem("v_mid"), sem("v_low")
        s_s, s_mx, s_ex, s_t, s_ph, s_pl, s_pv = (sem("scores"), sem("neg_max"), sem("exps"), sem("probT"),
                                                  sem("probT_hi"), sem("probT_lo"), sem("pv"))
        s_os, s_on, s_oT, s_oh, s_ol, s_o, s_x2 = (sem("o_sum"), sem("o_norm"), sem("oT"), sem("oT_hi"), sem("oT_lo"),
                                                   sem("wo_out"), sem("residual"))
        s_mv2, s_ve2, s_rs2, s_xn2, s_xT2 = (sem("mean_var_f"), sem("var_eps_f"), sem("inv_std_f"),
                                                    sem("xn_f"), sem("xnT_f"))
        s_fh, s_fl, s_fh2, s_fl2 = sem("ffnT_hi_tile"), sem("ffnT_lo_tile"), sem("ffnT_hi"), sem("ffnT_lo")
        s_gz, s_nz, s_ez, s_rt, s_w, s_wT, s_wTs = (sem("gate_psum"), sem("neg_z"), sem("exp_neg_z"), sem("route_step"),
                                                    sem("weight"), sem("weightT_psum"), sem("weightT"))
        s_bdp, s_bds, s_first = sem("bd_psum"), sem("bd_term"), sem("shared_and_bias")
        s_u, s_ge, s_ah, s_al, s_y, s_ys, s_add, s_moeT, s_res = (
            sem("up"), sem("gelu"), sem("act_hi"), sem("act_lo"), sem("down"), sem("y_scaled"), sem("moe_add"),
            sem("moeT"), sem("result"))

        def wait(engine, semaphore, value):
            if not (isinstance(value, int) and value <= 0):
                engine.wait_ge(semaphore, value)

        def at(i, size):
            return bass.ds(i * size, size)

        def for_groups(engine, step, steps):
            for u in range(steps):
                step(0, u, True)
            with engine.Fori(1, NG - 1) as i:
                for u in range(steps):
                    step(i, u, True)
            for u in range(steps):
                step(NG - 1, u, False)

        block = ctx.enter_context(nc.Block())

        @block.sync
        def _(sp):
            xv = x_in.rearrange("b p d -> p b d")
            sp.dma_start(x[:, 0:GB, :], xv[:, 0:GB, :]).then_inc(s_x0, 16)
            sp.dma_start(ctxT[:, 0:TOK], ctxT_in[:, 0:TOK]).then_inc(s_x0, 16)
            sp.dma_start(wqkvo[:, :], wqkvo_in).then_inc(s_wa, 16)
            sp.dma_start(identf[:, :], ident_in).then_inc(s_ident, 16)
            sp.dma_start(mask8[:, :], mask_in).then_inc(s_mask, 16)
            sp.dma_start(gates[:, 0:1], g_x_in.partition_broadcast(128)).then_inc(s_small, 16)
            sp.dma_start(x[:, GB:NB, :], xv[:, GB:NB, :]).then_inc(s_xrest, 16)
            sp.dma_start(ctxT[:, TOK:NB * SEQ], ctxT_in[:, TOK:NB * SEQ]).then_inc(s_xrest, 16)

            def store_k(j):
                sp.wait_ge(s_kl, j + 1)
                sp.dma_start(qk_dram[2:4, :, at(j, TOK)].rearrange("a r t -> r a t"),
                             k_parts.bitcast(f32)).then_inc(s_k_out, 16)
                sp.wait_ge(s_k_out, 16 * (j + 1))

            def store_q(j):
                sp.wait_ge(s_ql, j + 1)
                for part, tile in ((1, q_lo), (0, q_hi)):
                    sp.dma_start(qk_dram[part, :, at(j, TOK)], tile.bitcast(f32)).then_inc(s_q_out, 16)
                sp.wait_ge(s_q_out, 32 * (j + 1))

            def load_k(j, h):
                first = j * TOK + h * 2 * SEQ
                for c, (_, part) in enumerate(PARTS):
                    for n in range(HU):
                        src = qk_dram[2 + part, :, bass.ds(first, 2 * SEQ)].rearrange(
                            "(g n d) t -> n d g t", g=UB, n=HU)[n]
                        p = DH * (HU * c + n)
                        sp.dma_start(k_pack[p:p + DH, h, :, n, :].bitcast(f32), src).then_inc(s_kpack[h], 16)

            def load_q(j, h):
                first = j * TOK + h * 2 * SEQ
                for c, (part, _) in enumerate(PARTS):
                    src = qk_dram[part, :, bass.ds(first, 2 * SEQ)].rearrange("(g r) t -> r g t", g=UB)
                    p = HU * DH * c
                    sp.dma_start(q_pack[p:p + HU * DH, h, :, :].bitcast(f32), src).then_inc(s_qpack[h], 16)

            store_k(0)
            sp.wait_ge(s_pool0, 2)
            load_k(0, 0)
            store_q(0)
            load_q(0, 0)
            load_q(0, 1)
            load_k(0, 1)
            sp.dma_start(gates[:, 1:2], g_f_in.partition_broadcast(128)).then_inc(s_small, 16)
            sp.dma_start(earlier[:, :], earlier_in.partition_broadcast(128)).then_inc(s_small, 16)
            sp.dma_start(gate_b[:, :], gate_b_in.partition_broadcast(128)).then_inc(s_small, 16)
            sp.dma_start(gate_w[:, :], gate_wT_in).then_inc(s_small, 16)
            sp.dma_start(bu[:, :], bu_in).then_inc(s_small, 16)
            sp.dma_start(bd[:, :], bd_in).then_inc(s_small, 16)
            with sp.Fori(1, NG) as j:
                store_k(j)
                sp.wait_ge(s_s, UN * (j - 1) + UN // 2)
                load_k(j, 0)
                store_q(j)
                load_q(j, 0)
                sp.wait_ge(s_s, UN * j)
                load_k(j, 1)
                load_q(j, 1)
            sp.wait_ge(s_s, NG * UN - UN // 2)

            def weights_round(j):
                sp.wait_ge(s_wTs, j + 1)
                sp.dma_start(w_dram[bass.ds(j, 1), :, :].rearrange("a e t -> (a e) t"),
                             weightT[1:E1, :]).then_inc(s_wt_out, 16)
                sp.wait_ge(s_wt_out, 16 * (j + 1))
                for e in range(E):
                    wait(sp, s_ys, E * (j - 1) + e + 1)
                    src = w_dram[bass.ds(j, 1), e, :].rearrange("a t -> (a t)").partition_broadcast(128)
                    sp.dma_start(weight_all[:, e, :], src).then_inc(s_wall, 16)

            weights_round(0)
            with sp.Fori(1, NG) as j:
                weights_round(j)
                sp.wait_ge(s_res, j)
                sp.dma_start(out_dram[at(j - 1, GB), :, :].rearrange("b p d -> p b d"), result[:, :, :]).then_inc(s_out, 16)
            sp.wait_ge(s_res, NG)
            sp.dma_start(out_dram[NB - GB:NB, :, :].rearrange("b p d -> p b d"), result[:, :, :]).then_inc(s_out, 16)
            sp.wait_ge(s_out, 16 * (NG + 1))

        @block.gpsimd
        def _(pool):
            g = nc.gpsimd
            g.memset(minus_half[:, :], -0.5).then_inc(s_pool0, 1)
            g.memset(k_pack[:, :, :, :, :].bitcast(f32), 0.0).then_inc(s_pool0, 1)
            g.memset(v_parts[:, :, :, VC - 1:VC], 1.0).then_inc(s_pool0, 1)
            g.memset(ones[:, :], 1.0).then_inc(s_pool0, 1)
            g.memset(e_const[:, :], float(np.e)).then_inc(s_pool0, 1)
            g.memset(weight[:, :, 0:1], SHARED_WEIGHT).then_inc(s_pool0, 1)
            g.memset(top_sum[:, :], 0.0).then_inc(s_out, 16)
            pool.wait_ge(s_pool0, 6)
            pool.wait_ge(s_mk, 1)

            def norm_and_context(j):
                pool.wait_ge(s_ve, j + 1)
                g.tensor_tensor(inv_std[:, :], var_eps[:, :], minus_half[:, :], ALU.pow).then_inc(s_pw, 1)
                pool.wait_ge(s_pw, j + 1)
                g.tensor_tensor(inv_std_open[:, :], inv_std[:, :], row_open[:, 0:1].broadcast_to([128, GB]),
                                ALU.mult).then_inc(s_rs, 1)
                pool.wait_ge(s_ch, j + 1)
                g.tensor_tensor(cT_lo, ctxT[:, at(j, TOK)], cT_hi.bitcast(f32), ALU.subtract).then_inc(s_cl, 1)

            def rows(a, n=TOK // DH):
                return a.rearrange("p (n d) -> p n d", n=n)

            def v_rounds(j):
                mid = v_parts[:, at(j, GB), :, DH:2 * DH].rearrange("p b h d -> p (b h) d")
                low = v_parts[:, at(j, GB), :, 2 * DH:3 * DH].rearrange("p b h d -> p (b h) d")
                pool.wait_ge(s_vr, j + 1)
                g.tensor_tensor(mid, rows(wqkvo[:, :]), rows(ones[:, :]), ALU.mult).then_inc(s_vm, 1)
                pool.wait_ge(s_vm, j + 1)
                g.tensor_tensor(low, rows(wqkvo[:, :]), mid, ALU.subtract).then_inc(s_vl, 1)

            def load_w(n, k):
                g.dma_start(w_raw[:, k:k + 1, :], wffn_in[:, bass.ds(n, 1), :]).then_inc(s_wraw[k], 16)

            def split_w(n, k, uses):
                pool.wait_ge(s_wraw[k], 16 * uses)
                hi, lo = w_hi[:, bass.ds(n, 1), :], w_lo[:, bass.ds(n, 1), :]
                g.tensor_tensor(hi, w_raw[:, k:k + 1, :], ones[:, :].rearrange("p (a n) -> p a n", a=1),
                                ALU.mult).then_inc(s_wh, 1)
                pool.wait_ge(s_wh, n + 1)
                g.tensor_tensor(lo, w_raw[:, k:k + 1, :], hi.bitcast(f32), ALU.subtract).then_inc(s_wl, 1)

            per_group = 2 * E1 // (NG - 1)

            def split_beside(k, last):
                for m in range(per_group):
                    n = k * per_group + m
                    split_w(n, m % 2, k * (per_group // 2) + m // 2 + 1)
                    if not (last and m >= per_group - 2):
                        pool.wait_ge(s_wl, n + 1)
                        load_w(n + 2, m % 2)

            norm_and_context(0)
            v_rounds(0)
            for k in range(2):
                load_w(k, k)
            with pool.Fori(0, NG - 2) as k:
                norm_and_context(k + 1)
                split_beside(k, False)
                v_rounds(k + 1)
            norm_and_context(NG - 1)
            split_beside(NG - 2, True)
            v_rounds(NG - 1)

            def inverse_std(j):
                pool.wait_ge(s_ve2, j + 1)
                g.tensor_tensor(inv_std[:, :], var_eps[:, :], minus_half[:, :], ALU.pow).then_inc(s_rs2, 1)

            def exp_gate(j):
                pool.wait_ge(s_nz, j + 1)
                g.tensor_tensor(exp_neg_z[:, :, :], e_const[:, :].rearrange("p (t e) -> p t e", t=GB), neg_z[:, :, :],
                                ALU.pow).then_inc(s_ez, 1)

            def add(i, e):
                pool.wait_ge(s_ys, E * i + e)
                wait(pool, s_add, E * i + e - 1)
                if e == 1:
                    pool.wait_ge(s_first, i + 1)
                g.tensor_tensor(moe[:, :], moe[:, :], y_scaled[:, e % 2, :], ALU.add).then_inc(s_add, 1)

            def stage_f(i, more):
                if more:
                    inverse_std(i + 1)
                for e in range(1, E1):
                    add(i, e)
                    if more and e == 3:
                        exp_gate(i + 1)

            inverse_std(0)
            exp_gate(0)
            stage_f(0, True)
            with pool.Fori(1, NG - 1) as i:
                stage_f(i, True)
            stage_f(NG - 1, False)

        @block.scalar
        def _(act_e):
            a = nc.scalar
            act_e.wait_ge(s_wa, 16)
            a.activation(wqkvo_hi[:, :], wqkvo[:, :], ACT.Copy).then_inc(s_wah, 1)

            def context_high(j):
                if not isinstance(j, int) or j:
                    act_e.wait_ge(s_xrest, 32)
                else:
                    act_e.wait_ge(s_x0, 32)
                wait(act_e, s_v, j)
                a.activation(cT_hi, ctxT[:, at(j, TOK)], ACT.Copy).then_inc(s_ch, 1)

            def k_high(j, bk):
                act_e.wait_ge(s_k, j + 1)
                wait(act_e, s_k_out, 16 * j)
                a.activation(k_hi, bk[:, :], ACT.Copy).then_inc(s_kh, 1)

            def xn_high(j, bk):
                act_e.wait_ge(s_xT, j + 1)
                a.activation(xnT_hi[:, :], bk[:, :], ACT.Copy).then_inc(s_xh, 1)

            def v_high(j, bk):
                act_e.wait_ge(s_v, j + 1)
                a.activation(v_parts[:, at(j, GB), :, 0:DH],
                             bk[:, :].rearrange("p (b h d) -> p b h d", b=GB, h=HEADS), ACT.Copy).then_inc(s_vh, 1)

            def q_high(j, bk):
                act_e.wait_ge(s_q, j + 1)
                wait(act_e, s_q_out, 32 * j)
                a.activation(q_hi, bk[:, :], ACT.Copy, scale=QSCALE).then_inc(s_qh, 1)

            context_high(0)
            xn_high(0, bank[0])
            k_high(0, bank[2])
            v_high(0, bank[3])
            q_high(0, bank[1])

            act_e.wait_ge(s_small, 16 * 7)
            a.activation(tanh_gates[:, :], gates[:, :], ACT.Tanh).then_inc(s_tanh, 1)
            a.activation(gate_hi[:, :], gate_w[:, :], ACT.Copy).then_inc(s_tanh, 1)

            def exps(n, u):
                act_e.wait_ge(s_mx, n + 1)
                wait(act_e, s_t, n - 1)
                for j in range(HU):
                    last = a.activation(prob[:, u % 2, j, :], bank[u % 4][:, SEQ * j:SEQ * (j + 1)], ACT.Exp,
                                        bias=neg_max[:, u % 4, j:j + 1])
                last.then_inc(s_ex, 1)

            def step(i, u, more):
                if u + 1 < UN or more:
                    exps(UN * i + u + 1, (u + 1) % UN)
                n = UN * i + u
                act_e.wait_ge(s_t, n + 1)
                wait(act_e, s_pv, n - 1)
                a.activation(probT_hi[:, u % 2, :], bank[4 + u % 2][:, :], ACT.Copy).then_inc(s_ph, 1)
                if u % UB == 1:
                    high_o(GB * i + u // UB - 1, (u // UB - 1) % 2)
                if more:
                    if u == 1:
                        context_high(i + 1)
                    if u == 3:
                        k_high(i + 1, bank[7])
                    if u == 4:
                        xn_high(i + 1, bank[7])
                    if u == 7:
                        q_high(i + 1, bank[7])
                    if u == 8:
                        v_high(i + 1, bank[7])
                else:
                    if u == 3:
                        tile_high(0, bank[7])
                    if u == 5:
                        keep_parts(0)
                    if u == 7:
                        weight_rows(0)

            def high_o(b, par):
                if isinstance(b, int) and b < 0:
                    return
                act_e.wait_ge(s_oT, b + 1)
                wait(act_e, s_o, b - 1)
                a.activation(oT_hi[:, par, :], bank[7][:, 0:SEQ], ACT.Copy).then_inc(s_oh, 1)

            def tile_high(j, bk):
                act_e.wait_ge(s_xT2, j + 1)
                wait(act_e, s_gz, j)
                a.activation(xnT_hi[:, :], bk[:, :], ACT.Copy).then_inc(s_fh, 1)

            def keep_parts(j):
                act_e.wait_ge(s_fh, j + 1)
                a.activation(ffnT_hi[:, at(j, TOK)], xnT_hi[:, :].bitcast(f32), ACT.Copy).then_inc(s_fh2, 1)
                act_e.wait_ge(s_fl, j + 1)
                a.activation(ffnT_lo[:, at(j, TOK)], xnT_lo[:, :].bitcast(f32), ACT.Copy).then_inc(s_fl2, 1)

            def weight_rows(j):
                act_e.wait_ge(s_wT, j + 1)
                wait(act_e, s_wt_out, 16 * j)
                wait(act_e, s_bdp, j)
                a.activation(weightT[:, :], bank[7][0:E1, :], ACT.Copy).then_inc(s_wTs, 1)

            exps(0, 0)
            for_groups(act_e, step, UN)
            high_o(NB - 1, 1)

            def bias_term(i):
                act_e.wait_ge(s_bdp, i + 1)
                wait(act_e, s_first, i)
                a.activation(bias_sum, bank[6][:, :], ACT.Copy).then_inc(s_bds, 1)

            def ffn_step(i, n, more):
                m = CH * i + n
                act_e.wait_ge(s_u, m + 1)
                wait(act_e, s_al, m - 3)
                a.activation(act[:, n % 4, :], bank[n % 4][:, :], ACT.Gelu, bias=bu[:, n:n + 1]).then_inc(s_ge, 1)
                if n:
                    high_act(m - 1, n - 1)
                if n == CH - 1:
                    high_act(m, n)
                if n == 4:
                    bias_term(i)
                if more and n == 12:
                    tile_high(i + 1, bank[6])
                if more and n == 18:
                    keep_parts(i + 1)
                if more and n == 31:
                    weight_rows(i + 1)

            def high_act(m, n):
                act_e.wait_ge(s_ge, m + 1)
                wait(act_e, s_down_of(m), m - 3)
                a.activation(act_hi[:, n % 4, :], act[:, n % 4, :], ACT.Copy).then_inc(s_ah, 1)

            def s_down_of(m):
                return s_y

            for_groups(act_e, ffn_step, CH)

        @block.vector
        def _(dve):
            v = nc.vector
            dve.wait_ge(s_mask, 16)
            v.tensor_copy(maskf[:, :], mask8[:, :]).then_inc(s_ib, 1)
            dve.wait_ge(s_ib, 1)
            v.reduce_max(row_open[:, :], maskf[:, :], AX.X).then_inc(s_mk, 1)
            v.tensor_scalar(mask_low[:, :], maskf[:, :], 1.0, MASKED, ALU.subtract, ALU.mult).then_inc(s_ib, 1)
            dve.wait_ge(s_mk, 1)
            dve.wait_ge(s_ib, 2)
            v.tensor_scalar(mask_bias[:, :], mask_low[:, :], row_open[:, 0:1], None, ALU.mult).then_inc(s_mk, 1)

            def norm_stats(i, smv, sve):
                for t in range(GB):
                    v.bn_stats(stats[:, t, :], x[:, at(i * GB + t, 1), :].rearrange("p a d -> p (a d)"))
                dve.drain()
                for t in range(GB):
                    v.bn_aggr(mean_var[:, t, :], stats[:, t, :]).then_inc(smv, 1)
                dve.wait_ge(smv, GB * i + GB)
                v.tensor_scalar(var_eps[:, :], mean_var[:, :, 1], EPS, None, ALU.add).then_inc(sve, 1)

            def norm_apply(i, scale, sxn):
                for t in range(GB):
                    v.tensor_scalar(xn[:, t, :], x[:, at(i * GB + t, 1), :].rearrange("p a d -> p (a d)"),
                                    mean_var[:, t, 0:1], scale[:, t:t + 1], ALU.subtract, ALU.mult).then_inc(sxn, 1)

            def norm_p(j):
                if not isinstance(j, int) or j:
                    dve.wait_ge(s_xrest, 32)
                else:
                    dve.wait_ge(s_x0, 32)
                norm_stats(j, s_mv, s_ve)

            def apply_p(j):
                dve.wait_ge(s_rs, j + 1)
                wait(dve, s_xT, j)
                norm_apply(j, inv_std_open, s_xn)

            def k_low(j, bk):
                dve.wait_ge(s_kh, j + 1)
                v.tensor_tensor(k_lo, bk[:, :], k_hi.bitcast(f32), ALU.subtract).then_inc(s_kl, 1)

            def xn_low(j, bk):
                dve.wait_ge(s_xh, j + 1)
                v.tensor_tensor(xnT_lo[:, :], bk[:, :], xnT_hi[:, :].bitcast(f32), ALU.subtract).then_inc(s_xl, 1)

            def v_low(j, bk):
                dve.wait_ge(s_vh, j + 1)
                wait(dve, s_vl, j)
                v.tensor_tensor(v_rest[:, :, :, :].rearrange("p b h d -> p (b h) d"),
                                bk[:, :].rearrange("p (n d) -> p n d", d=DH),
                                v_parts[:, at(j, GB), :, 0:DH].rearrange("p b h d -> p (b h) d"),
                                ALU.subtract).then_inc(s_vr, 1)

            def q_low(j, bk):
                dve.wait_ge(s_qh, j + 1)
                v.scalar_tensor_tensor(q_lo, bk[:, :], QSCALE, q_hi.bitcast(f32), ALU.mult,
                                       ALU.subtract).then_inc(s_ql, 1)

            norm_p(0)
            dve.wait_ge(s_wah, 1)
            v.tensor_tensor(wqkvo_lo[:, :], wqkvo[:, :], wqkvo_hi[:, :].bitcast(f32), ALU.subtract).then_inc(s_wal, 1)
            apply_p(0)
            dve.wait_ge(s_ident, 16)
            v.tensor_copy(identb[:, :], identf[:, :]).then_inc(s_ib, 1)
            dve.wait_ge(s_wal, 1)
            xn_low(0, bank[0])
            k_low(0, bank[2])
            v_low(0, bank[3])
            q_low(0, bank[1])
            dve.wait_ge(s_tanh, 2)
            v.tensor_tensor(gate_lo[:, :], gate_w[:, :], gate_hi[:, :].bitcast(f32), ALU.subtract).then_inc(s_wal, 1)

            def maxima(n, u):
                dve.wait_ge(s_s, n + 1)
                v.tensor_reduce(neg_max[:, u % 4, :], bank[u % 4][:, :].rearrange("p (j k) -> p j k", j=HU), AX.X,
                                ALU.max, negate=True).then_inc(s_mx, 1)

            def normalize(b, par):
                if isinstance(b, int) and b < 0:
                    return
                dve.wait_ge(s_pv, UB * b + UB)
                o = bank[6][:, 0:HEADS * VC].rearrange("p (h c) -> p h c", c=VC)
                v.tensor_reduce(o_sum[:, :, :], o[:, :, 0:3 * DH].rearrange("p h (c d) -> p h d c", c=3), AX.X,
                                ALU.add).then_inc(s_os, 1)
                v.reciprocal(inv_sum[:, :], o[:, :, VC - 1]).then_inc(s_os, 1)
                dve.wait_ge(s_os, 2 * b + 2)
                v.tensor_tensor(o_norm[:, par, :, :], o_sum[:, :, :],
                                inv_sum[:, :].rearrange("p (h a) -> p h a", a=1).broadcast_to([128, HEADS, DH]),
                                ALU.mult).then_inc(s_on, 1)

            def low_o(b, par):
                if isinstance(b, int) and b < 0:
                    return
                dve.wait_ge(s_oh, b + 1)
                v.tensor_tensor(oT_lo[:, par, :], bank[7][:, 0:SEQ], oT_hi[:, par, :].bitcast(f32),
                                ALU.subtract).then_inc(s_ol, 1)

            def residual(b, par):
                if isinstance(b, int) and b < 0:
                    return
                dve.wait_ge(s_o, b + 1)
                xb = x[:, at(b, 1), :].rearrange("p a d -> p (a d)")
                v.scalar_tensor_tensor(xb, bank[7][:, SEQ:SEQ + D], tanh_gates[:, 0:1], xb, ALU.mult,
                                       ALU.add).then_inc(s_x2, 1)

            def step(i, u, more):
                if u + 2 < UN or more:
                    maxima(UN * i + u + 2, (u + 2) % UN)
                n = UN * i + u
                dve.wait_ge(s_ph, n + 1)
                v.tensor_tensor(probT_lo[:, u % 2, :], bank[4 + u % 2][:, :], probT_hi[:, u % 2, :],
                                ALU.subtract).then_inc(s_pl, 1)
                b, par = GB * i + u // UB - 1, (u // UB - 1) % 2
                if u % UB == 0:
                    normalize(b, par)
                if u % UB == 1:
                    low_o(b, par)
                if u % UB == 2:
                    residual(b, par)
                if more:
                    if u == 0:
                        norm_p(i + 1)
                    if u == 2:
                        apply_p(i + 1)
                    if u == 3:
                        k_low(i + 1, bank[7])
                    if u == 4:
                        xn_low(i + 1, bank[7])
                    if u == 7:
                        q_low(i + 1, bank[7])
                    if u == 8:
                        v_low(i + 1, bank[7])
                else:
                    if u == 0:
                        norm_stats(0, s_mv2, s_ve2)
                    if u == 2:
                        dve.wait_ge(s_rs2, 1)
                        norm_apply(0, inv_std, s_xn2)
                    if u == 3:
                        xn_parts(0, bank[7])
                    if u == 4:
                        gate_logits(0)
                    if u == 6:
                        for part in range(5):
                            route(0, part)

            def xn_parts(j, bk):
                dve.wait_ge(s_fh, j + 1)
                v.tensor_tensor(xnT_lo[:, :], bk[:, :], xnT_hi[:, :].bitcast(f32), ALU.subtract).then_inc(s_fl, 1)

            def gate_logits(j):
                dve.wait_ge(s_gz, j + 1)
                v.scalar_tensor_tensor(neg_z[:, :, :], bank[7][:, 0:GB * E].rearrange("p (t e) -> p t e", t=GB), -1.0,
                                       gate_b[:, :].rearrange("p (a e) -> p a e", a=1).broadcast_to([128, GB, E]),
                                       ALU.mult, ALU.subtract).then_inc(s_nz, 1)

            def route(j, part):
                steps = 9
                if part == 0:
                    dve.wait_ge(s_ez, j + 1)
                    v.tensor_scalar(sig_den[:, :, :], exp_neg_z[:, :, :], 1.0, None, ALU.add).then_inc(s_rt, 1)
                    dve.wait_ge(s_rt, steps * j + 1)
                    v.reciprocal(sig[:, :, :], sig_den[:, :, :]).then_inc(s_rt, 1)
                if part == 1:
                    dve.wait_ge(s_rt, steps * j + 2)
                    this = sig[:, :, :].rearrange("p t (e a) -> p t e a", a=1).broadcast_to([128, GB, E, E])
                    other = sig[:, :, :].rearrange("p t (a e) -> p t a e", a=1).broadcast_to([128, GB, E, E])
                    v.tensor_tensor(beats[:, :, :, :], other, this, ALU.is_gt).then_inc(s_rt, 1)
                    v.tensor_tensor(ties[:, :, :, :], other, this, ALU.is_equal).then_inc(s_rt, 1)
                    dve.wait_ge(s_rt, steps * j + 4)
                    flat = ties[:, :, :, :].rearrange("p t e f -> p t (e f)")
                    before = earlier[:, :].rearrange("p (a n) -> p a n", a=1).broadcast_to([128, GB, E * E])
                    v.tensor_tensor(flat, flat, before, ALU.mult).then_inc(s_rt, 1)
                if part == 2:
                    dve.wait_ge(s_rt, steps * j + 5)
                    v.tensor_tensor(beats[:, :, :, :], beats[:, :, :, :], ties[:, :, :, :], ALU.add).then_inc(s_rt, 1)
                    dve.wait_ge(s_rt, steps * j + 6)
                    v.tensor_reduce(rank[:, :, :], beats[:, :, :, :], AX.X, ALU.add).then_inc(s_rt, 1)
                if part == 3:
                    dve.wait_ge(s_rt, steps * j + 7)
                    v.scalar_tensor_tensor(sig_top[:, :, :], rank[:, :, :], 2.0, sig[:, :, :], ALU.is_lt,
                                           ALU.mult).then_inc(s_rt, 1)
                    dve.wait_ge(s_rt, steps * j + 8)
                    v.tensor_reduce(top_sum[:, :], sig_top[:, :, :], AX.X, ALU.add).then_inc(s_rt, 1)
                    dve.wait_ge(s_rt, steps * j + 9)
                    v.tensor_scalar(top_sum[:, :], top_sum[:, :], TINY, None, ALU.add).then_inc(s_w, 1)
                if part == 4:
                    dve.wait_ge(s_w, 3 * j + 1)
                    v.reciprocal(inv_top[:, :], top_sum[:, :]).then_inc(s_w, 1)
                    dve.wait_ge(s_w, 3 * j + 2)
                    wait(dve, s_wT, j)
                    v.tensor_tensor(weight[:, :, 1:E1], sig_top[:, :, :],
                                    inv_top[:, :].rearrange("p (t a) -> p t a", a=1).broadcast_to([128, GB, E]),
                                    ALU.mult).then_inc(s_w, 1)

            maxima(0, 0)
            maxima(1, 1)
            for_groups(dve, step, UN)
            normalize(NB - 1, 1)
            low_o(NB - 1, 1)
            residual(NB - 1, 1)

            def combine(i, e):
                dve.wait_ge(s_y, CH * i + FC * e + FC)
                y = bank[4 + e % 2]
                if e == 0:
                    dve.wait_ge(s_bds, i + 1)
                    wait(dve, s_moeT, i)
                    v.scalar_tensor_tensor(moe[:, :], y[:, :], SHARED_WEIGHT, bias_sum, ALU.mult,
                                           ALU.add).then_inc(s_first, 1)
                else:
                    dve.wait_ge(s_wall, 16 * (E * i + E))
                    wait(dve, s_add, E * i + e - 2)
                    v.tensor_tensor(y_scaled[:, e % 2, :], y[:, :], weight_all[:, e - 1, :], ALU.mult).then_inc(s_ys, 1)

            def finish(i):
                if isinstance(i, int) and i < 0:
                    return
                dve.wait_ge(s_moeT, i + 1)
                dve.wait_ge(s_out, 16 * (i + 1))
                v.scalar_tensor_tensor(result[:, :, :], bank[7][:, :].rearrange("p (b d) -> p b d", b=GB),
                                       tanh_gates[:, 1:2], x[:, at(i, GB), :], ALU.mult, ALU.add).then_inc(s_res, 1)

            def ffn_step(i, n, more):
                m = CH * i + n
                dve.wait_ge(s_ah, m + 1)
                wait(dve, s_y, m - 3)
                v.tensor_tensor(act_lo[:, n % 4, :], act[:, n % 4, :], act_hi[:, n % 4, :].bitcast(f32),
                                ALU.subtract).then_inc(s_al, 1)
                if n == 8:
                    combine(i, 0)
                if n % FC == 1 and n > 2 * FC:
                    combine(i, n // FC - 1)
                if n == 7:
                    finish(i - 1)
                if n == CH - 1:
                    combine(i, E)
                if more and n == 2:
                    norm_stats(i + 1, s_mv2, s_ve2)
                if more and n == 6:
                    dve.wait_ge(s_rs2, i + 2)
                    norm_apply(i + 1, inv_std, s_xn2)
                if more and n == 14:
                    xn_parts(i + 1, bank[6])
                if more and n == 17:
                    gate_logits(i + 1)
                if more and 23 <= n < 28:
                    route(i + 1, n - 23)

            for_groups(dve, ffn_step, CH)
            finish(NG - 1)

        @block.tensor
        def _(pe):
            mm = nc.tensor.matmul

            def three(out, w_h, w_l, r_h, r_l, start=True, stop=True):
                mm(out, w_h, r_h, start=start, stop=False)
                mm(out, w_l, r_h, start=False, stop=False)
                return mm(out, w_h, r_l, start=False, stop=stop)

            def wa(part, k):
                return part[:, D * k:D * (k + 1)]

            pe.wait_ge(s_ident, 16)
            pe.wait_ge(s_wah, 1)

            def project_k(j, bk):
                pe.wait_ge(s_cl, j + 1)
                three(bk[:, :], wa(wqkvo_hi, 1), wa(wqkvo_lo, 1), cT_hi, cT_lo).then_inc(s_k, 1)

            def transpose_xn(j, bk):
                pe.wait_ge(s_xn, GB * j + GB)
                for t in range(GB):
                    last = nc.tensor.transpose(bk[:, D * t:D * (t + 1)], xn[:, t, :], identf[:, :])
                last.then_inc(s_xT, 1)

            def project_v(j, bk):
                for t in range(GB):
                    c = slice(SEQ * t, SEQ * (t + 1))
                    last = three(bk[:, c], cT_hi[:, c], cT_lo[:, c], wa(wqkvo_hi, 2), wa(wqkvo_lo, 2))
                last.then_inc(s_v, 1)

            def project_q(j, bk):
                pe.wait_ge(s_xl, j + 1)
                three(bk[:, :], wa(wqkvo_hi, 0), wa(wqkvo_lo, 0), xnT_hi[:, :], xnT_lo[:, :]).then_inc(s_q, 1)

            transpose_xn(0, bank[0])
            pe.wait_ge(s_wal, 1)
            project_k(0, bank[2])
            project_v(0, bank[3])
            project_q(0, bank[1])

            def scores(i, u):
                b, g = u // UB, u % UB
                h = b // 2
                if u % (UN // 2) == 0:
                    pe.wait_ge(s_qpack[h], 16 * len(PARTS) * (i + 1))
                    pe.wait_ge(s_kpack[h], 16 * len(PARTS) * HU * (i + 1))
                out = bank[u % 4]
                t = slice(SEQ * (b % 2), SEQ * (b % 2 + 1))
                out4 = out[:, :].rearrange("p (j k) -> p j k", j=HU)
                mm(out4, q_pack[:, h, g, t], k_pack[0:KR, h, g, :, t], start=True, stop=False)
                mm(out4, identb[:, :],
                   mask_bias[:, :].rearrange("p (a k) -> p a k", a=1).broadcast_to([128, HU, SEQ]),
                   start=False, stop=True).then_inc(s_s, 1)

            def pv(i, u):
                b, g = u // UB, u % UB
                n = UN * i + u
                pe.wait_ge(s_pl, n + 1)
                if u == 0:
                    pe.wait_ge(s_vl, i + 1)
                if g == 0:
                    wait(pe, s_os, 2 * (GB * i + b))
                for j in range(HU):
                    h = HU * g + j
                    out = bank[6][:, VC * h:VC * (h + 1)]
                    rhs = v_parts[:, at(GB * i + b, 1), h, :].rearrange("p a c -> p (a c)")
                    mm(out, probT_hi[:, u % 2, SEQ * j:SEQ * (j + 1)], rhs, start=True, stop=False)
                    last = mm(out, probT_lo[:, u % 2, SEQ * j:SEQ * (j + 1)], rhs, start=False, stop=True)
                last.then_inc(s_pv, 1)

            def o_transpose(b, par):
                if isinstance(b, int) and b < 0:
                    return
                pe.wait_ge(s_on, b + 1)
                wait(pe, s_x2, b)
                nc.tensor.transpose(bank[7][:, 0:SEQ], o_norm[:, par, :, :].rearrange("p h d -> p (h d)"),
                                    identf[:, :]).then_inc(s_oT, 1)

            def wo(b, par):
                if isinstance(b, int) and b < 0:
                    return
                pe.wait_ge(s_ol, b + 1)
                three(bank[7][:, SEQ:SEQ + D], oT_hi[:, par, :], oT_lo[:, par, :], wa(wqkvo_hi, 3),
                      wa(wqkvo_lo, 3)).then_inc(s_o, 1)

            def ffn_transpose(j, bk):
                pe.wait_ge(s_xn2, GB * j + GB)
                wait(pe, s_bds, j)
                for t in range(GB):
                    last = nc.tensor.transpose(bk[:, D * t:D * (t + 1)], xn[:, t, :], identf[:, :])
                last.then_inc(s_xT2, 1)

            def gate(j):
                pe.wait_ge(s_fl, j + 1)
                wait(pe, s_res, j - 1)
                for t in range(GB):
                    c = slice(SEQ * t, SEQ * (t + 1))
                    last = three(bank[7][:, E * t:E * (t + 1)], xnT_hi[:, c], xnT_lo[:, c], gate_hi[:, :], gate_lo[:, :])
                last.then_inc(s_gz, 1)

            def weight_transpose(j):
                pe.wait_ge(s_w, 3 * j + 3)
                for t in range(GB):
                    last = nc.tensor.transpose(bank[7][0:E1, SEQ * t:SEQ * (t + 1)], weight[:, t, :], identf[:, :])
                last.then_inc(s_wT, 1)

            def step(i, u, more):
                n = UN * i + u
                wait(pe, s_ex, n)
                if u + 3 < UN:
                    scores(i, u + 3)
                elif more:
                    scores(i + 1, u + 3 - UN)
                pe.wait_ge(s_ex, n + 1)
                wait(pe, s_pl, n - 1)
                for j in range(HU):
                    last = nc.tensor.transpose(bank[4 + u % 2][:, SEQ * j:SEQ * (j + 1)], prob[:, u % 2, j, :],
                                               identf[:, :])
                last.then_inc(s_t, 1)
                b, par = GB * i + u // UB - 1, (u // UB - 1) % 2
                if u % UB == 1:
                    if more and u == 5:
                        pe.wait_ge(s_xl, i + 2)
                    if more and u == 9:
                        pe.wait_ge(s_vr, i + 2)
                    if not more and u == 5:
                        pe.wait_ge(s_nz, 1)
                    if not more and u == 9:
                        pe.wait_ge(s_wTs, 1)
                    o_transpose(b, par)
                if u % UB == 2:
                    wo(b, par)
                if more:
                    if u == 3:
                        wait(pe, s_x2, b + 1)
                        project_k(i + 1, bank[7])
                    if u == 4:
                        pe.wait_ge(s_kl, i + 2)
                        transpose_xn(i + 1, bank[7])
                    if u == 7:
                        wait(pe, s_x2, b + 1)
                        project_q(i + 1, bank[7])
                    if u == 8:
                        pe.wait_ge(s_ql, i + 2)
                        project_v(i + 1, bank[7])
                else:
                    if u == 3:
                        wait(pe, s_x2, b + 1)
                        ffn_transpose(0, bank[7])
                    if u == 4:
                        pe.wait_ge(s_wal, 2)
                        gate(0)
                    if u == 7:
                        wait(pe, s_x2, b + 1)
                        weight_transpose(0)
                if u:
                    pv(i, u - 1)
                elif not (isinstance(i, int) and i == 0):
                    pv(i - 1, UN - 1)

            pe.wait_ge(s_mk, 2)
            pe.wait_ge(s_ib, 3)
            pe.wait_ge(s_vl, 1)
            pe.wait_ge(s_kl, 1)
            pe.wait_ge(s_ql, 1)
            pe.wait_ge(s_pool0, 6)
            for u in range(3):
                scores(0, u)
            for_groups(pe, step, UN)

            def bias_term(i):
                pe.wait_ge(s_wTs, i + 1)
                pe.wait_ge(s_fh2, i + 1)
                mm(bank[6][:, :], bd[:, :], weightT[:, :], start=True, stop=True).then_inc(s_bdp, 1)

            def up(i, n):
                m = CH * i + n
                e, c = n // FC, n % FC
                wait(pe, s_ge, m - 3)
                if n == 0:
                    pe.wait_ge(s_fl2, i + 1)
                k = slice(D * c, D * (c + 1))
                three(bank[n % 4][:, :], w_hi[:, e, k], w_lo[:, e, k], ffnT_hi[:, at(i, TOK)],
                      ffnT_lo[:, at(i, TOK)]).then_inc(s_u, 1)

            def down(i, n):
                m = CH * i + n
                e, c = n // FC, n % FC
                pe.wait_ge(s_al, m + 1)
                if c == 0:
                    wait(pe, s_ys, E * i + e - 2 if e else E * i)
                    if e == 2:
                        pe.wait_ge(s_first, i + 1)
                k = slice(D * c, D * (c + 1))
                three(bank[4 + e % 2][:, :], w_hi[:, E1 + e, k], w_lo[:, E1 + e, k], act_hi[:, n % 4, :],
                      act_lo[:, n % 4, :], start=(c == 0), stop=(c == FC - 1)).then_inc(s_y, 1)

            def moe_transpose(i):
                if isinstance(i, int) and i < 0:
                    return
                pe.wait_ge(s_add, E * i + E)
                pe.wait_ge(s_wTs, min(NG, i + 2) if isinstance(i, int) else i + 2)
                for t in range(GB):
                    last = nc.tensor.transpose(bank[7][:, D * t:D * (t + 1)], moe[:, SEQ * t:SEQ * (t + 1)], identf[:, :])
                last.then_inc(s_moeT, 1)

            def ffn_step(i, n, more):
                if n + 3 < CH:
                    up(i, n + 3)
                elif more:
                    up(i + 1, n + 3 - CH)
                down(i, n)
                if n == 4:
                    moe_transpose(i - 1)
                if more and n == 8:
                    ffn_transpose(i + 1, bank[6])
                if more and n == 13:
                    gate(i + 1)
                if more and n == 28:
                    weight_transpose(i + 1)
                if n == 0:
                    bias_term(i)

            pv(NG - 1, UN - 1)
            pe.wait_ge(s_wl, 2 * E1)
            pe.wait_ge(s_ex, NG * UN)
            for n in range(2):
                up(0, n)
            o_transpose(NB - 1, 1)
            up(0, 2)
            wo(NB - 1, 1)
            pe.wait_ge(s_x2, NB)
            for_groups(pe, ffn_step, CH)
            moe_transpose(NG - 1)


def kernel(x, ctx_1024, mask_SxS2_bk0, g_xattn, g_ffn, L0_xattn_Wq, L0_xattn_Wk, L0_xattn_Wv, L0_xattn_Wo,
           L0_ffn_gate_w, L0_ffn_gate_bias, L0_ffn_Wu, L0_ffn_bu, L0_ffn_Wd, L0_ffn_bd, L0_ffn_sWu, L0_ffn_sbu,
           L0_ffn_sWd, L0_ffn_sbd):
    import concourse.bacc as bacc
    from concourse.bass_utils import run_bass_kernel_spmd

    def host(a):
        return np.ascontiguousarray(np.asarray(a))

    x = host(x)
    NB, SEQ, D = x.shape
    E, F = host(L0_ffn_bu).shape
    ctxT = host(host(ctx_1024).reshape(NB * SEQ, D).T)
    wqkvo = host(np.stack([host(w).T for w in (L0_xattn_Wq, L0_xattn_Wk, L0_xattn_Wv, L0_xattn_Wo)], 1).reshape(D, 4 * D))
    wu = np.concatenate([host(L0_ffn_sWu)[None], host(L0_ffn_Wu)], 0)
    wd = np.concatenate([host(L0_ffn_sWd)[None], host(L0_ffn_Wd)], 0)
    up = wu.transpose(2, 0, 1)
    down = wd.reshape(E + 1, D, F // 128, 128).transpose(3, 0, 2, 1).reshape(128, E + 1, F)
    wffn = host(np.concatenate([up, down], 1))
    bu = host(np.concatenate([host(L0_ffn_sbu)[None], host(L0_ffn_bu)], 0).reshape(-1, 128).T)
    bd = host(np.concatenate([host(L0_ffn_sbd)[None], host(L0_ffn_bd)], 0))
    arrays = {
        "x_in": x, "ctxT_in": ctxT, "mask_in": host(mask_SxS2_bk0), "g_x_in": host(g_xattn),
        "g_f_in": host(g_ffn), "wqkvo_in": wqkvo, "wffn_in": wffn, "bu_in": bu, "bd_in": bd,
        "gate_wT_in": host(host(L0_ffn_gate_w).T), "gate_b_in": host(L0_ffn_gate_bias),
        "ident_in": np.eye(128, dtype=np.float32),
        "earlier_in": np.tril(np.ones((E, E), np.float32), -1).reshape(-1),
    }
    nc = bacc.Bacc("TRN2", target_bir_lowering=False, num_devices=1)
    args = [nc.dram_tensor(n, a.shape, mybir.dt.from_np(a.dtype), kind="ExternalInput").ap() for n, a in arrays.items()]
    out = nc.dram_tensor("out", (NB, SEQ, D), mybir.dt.float32, kind="ExternalOutput").ap()
    build(nc, *args, out)
    r = run_bass_kernel_spmd(nc, [arrays], core_ids=[0])
    return r.results[0]["out"]
```

```python
from contextlib import ExitStack

import concourse.bass as bass
import concourse.mybir as mybir
import numpy as np


def build(nc, x_in, ctxT_in, mask_in, g_x_in, g_f_in, wqkvo_in, wffn_in, bu_in, bd_in, gate_wT_in, gate_b_in,
          ident_in, earlier_in, out_dram):
    f32, f32r, bf16, fp16, u8 = (mybir.dt.float32, mybir.dt.float32r, mybir.dt.bfloat16, mybir.dt.float16,
                                 mybir.dt.uint8)
    ALU, ACT, AX = mybir.AluOpType, mybir.ActivationFunctionType, mybir.AxisListType

    NB, SEQ, D = x_in.shape
    HEADS, DH = 16, D // 16
    E1 = wffn_in.shape[1] // 2
    E = E1 - 1
    GB = 4
    NG = NB // GB
    TOK = GB * SEQ
    HU = 4
    UB = HEADS // HU
    UN = GB * UB
    PARTS = ((0, 0), (1, 0), (0, 1))
    KR = len(PARTS) * HU * DH
    VC = 3 * DH + 1
    FC = wffn_in.shape[2] // D
    CH = E1 * FC
    EPS, MASKED, TINY = 1e-5, 1e9, 1e-6
    QSCALE = float(1.0 / np.sqrt(np.float32(DH)))
    SHARED_WEIGHT = 0.1

    qk_dram = nc.dram_tensor("qk_dram", (4, D, NB * SEQ), f32, kind="Internal").ap()
    w_dram = nc.dram_tensor("w_dram", (NG, E, TOK), f32, kind="Internal").ap()

    ctx = ExitStack()
    with ctx:
        def sb(name, shape, dt):
            return ctx.enter_context(nc.sbuf_tensor(name, shape, dt))

        def sem(name):
            return ctx.enter_context(nc.semaphore(name))

        bank = [ctx.enter_context(nc.psum_tensor(f"bank{i}", [128, 512], f32)) for i in range(8)]

        identf = sb("identf", [128, 128], f32)
        identb = sb("identb", [128, 128], bf16)
        earlier = sb("earlier", [128, E * E], f32)
        ones = sb("ones", [128, 512], f32)
        minus_half = sb("minus_half", [128, GB], f32)
        e_const = sb("e_const", [128, GB * E], f32)
        mask8 = sb("mask8", [128, SEQ], u8)
        mask_bias = sb("mask_bias", [128, SEQ], bf16)
        row_open = sb("row_open", [128, 1], f32)
        gates = sb("gates", [128, 2], f32)
        tanh_gates = sb("tanh_gates", [128, 2], f32)
        wqkvo = sb("wqkvo", [128, 4 * D], f32)
        wqkvo_hi = sb("wqkvo_hi", [128, 4 * D], f32r)
        wqkvo_lo = sb("wqkvo_lo", [128, 4 * D], f32r)
        gate_w = sb("gate_w", [128, E], f32)
        gate_hi = sb("gate_hi", [128, E], f32r)
        gate_lo = sb("gate_lo", [128, E], f32r)
        gate_b = sb("gate_b", [128, E], f32)
        bu = sb("bu", [128, CH], f32)
        bd = sb("bd", [E1, D], f32)
        w_raw = sb("w_raw", [128, 2, 512], f32)
        w_hi = sb("w_hi", [128, 2 * E1, 512], f32r)
        w_lo = sb("w_lo", [128, 2 * E1, 512], f32r)

        x = sb("x", [128, NB, D], f32)
        ctxT = sb("ctxT", [128, NB * SEQ], f32)
        stats = sb("stats", [128, GB, 6], f32)
        mean_var = sb("mean_var", [128, GB, 2], f32)
        var_eps = sb("var_eps", [128, GB], f32)
        inv_std = sb("inv_std", [128, GB], f32)
        inv_std_open = sb("inv_std_open", [128, GB], f32)
        xn = sb("xn", [128, GB, D], f32)
        xnT_hi = sb("xnT_hi", [128, TOK], f32r)
        xnT_lo = sb("xnT_lo", [128, TOK], f32r)
        arena = sb("arena", [128, 4, 4 * TOK], f32r)
        q_hi, q_lo, k_hi, k_lo = (arena[:, a, 0:TOK] for a in range(4))
        k_parts = arena[:, 2:4, 0:TOK]
        cT_hi, cT_lo = arena[:, 0, TOK:2 * TOK], arena[:, 1, TOK:2 * TOK]
        act_hi = arena[:, 0, :].rearrange("p (s n) -> p s n", s=4)
        act_lo = arena[:, 1, :].rearrange("p (s n) -> p s n", s=4)
        ffnT_hi, ffnT_lo = arena[:, 2, :], arena[:, 3, :]
        v_parts = sb("v_parts", [128, NB, HEADS, VC], bf16)
        q_pack = sb("q_pack", [KR, 2, UB, 2 * SEQ], f32r)
        k_pack = sb("k_pack", [128, 2, UB, HU, 2 * SEQ], f32r)
        neg_max = sb("neg_max", [128, 4, HU], f32)
        weight_all = k_pack[:, 0, :, :, :].rearrange("p g j k -> p (g j k)").bitcast(f32).rearrange(
            "p (e t) -> p e t", e=E)
        prob = sb("prob", [128, 2, HU, SEQ], f32)
        maskf, mask_low = prob[:, 0, 0, :], prob[:, 0, 1, :]
        v_rest = wqkvo[:, :]
        y_scaled = prob[:, :, :, :].rearrange("p a b c -> p a (b c)")
        probT_hi = sb("probT_hi", [128, 2, HU * SEQ], fp16)
        probT_lo = sb("probT_lo", [128, 2, HU * SEQ], fp16)
        bias_sum = probT_hi[:, :, :].rearrange("p a n -> p (a n)").bitcast(f32)
        o_sum = sb("o_sum", [128, HEADS, DH], f32)
        inv_sum = sb("inv_sum", [128, HEADS], f32)
        o_norm = sb("o_norm", [128, 2, HEADS, DH], f32)
        oT_hi = sb("oT_hi", [128, 2, SEQ], f32r)
        oT_lo = sb("oT_lo", [128, 2, SEQ], f32r)
        neg_z = sb("neg_z", [128, GB, E], f32)
        exp_neg_z = sb("exp_neg_z", [128, GB, E], f32)
        sig_den = sb("sig_den", [128, GB, E], f32)
        sig = sb("sig", [128, GB, E], f32)
        compare = wqkvo[:, :].rearrange("p (a t e f) -> p a t e f", a=2, t=GB, e=E)
        beats, ties = compare[:, 0], compare[:, 1]
        rank = sb("rank", [128, GB, E], f32)
        sig_top = sb("sig_top", [128, GB, E], f32)
        top_sum = sb("top_sum", [128, GB], f32)
        inv_top = sb("inv_top", [128, GB], f32)
        weight = sb("weight", [128, GB, E1], f32)
        weightT = sb("weightT", [E1, TOK], f32)
        act = ctxT[:, :].rearrange("p (s n) -> p s n", s=4)
        moe = w_raw[:, 1, :]
        result = w_raw[:, 0, :].rearrange("p (b d) -> p b d", b=GB)

        s_mask, s_ident, s_small, s_wa, s_x0, s_c0, s_xrest = sem("mask_in"), sem("ident_in"), sem("small_in"), sem("wa_in"), sem("x0_in"), sem("ctx0_in"), sem("xrest_in")
        s_wraw = [sem("wraw_even"), sem("wraw_odd")]
        s_k_out, s_q_out = sem("k_out"), sem("q_out")
        s_qpack = [sem("q_pack_even"), sem("q_pack_odd")]
        s_kpack, s_kpack_first = [sem("k_pack_even"), sem("k_pack_odd")], sem("k_pack_first")
        s_wt_out, s_wall, s_out = sem("weightT_out"), sem("weight_all_in"), sem("out")
        s_pool0, s_mk, s_wah, s_wal, s_tanh, s_ib = (sem("pool_constants"), sem("mask_done"), sem("wa_hi"), sem("wa_lo"),
                                                    sem("tanh_done"), sem("identb_done"))
        s_xc = sem("x_minus_mean")
        s_kzero = sem("k_pack_zero")
        s_wh, s_wl = sem("ffn_w_hi"), sem("ffn_w_lo")
        s_mv, s_ve, s_pw, s_rs = sem("mean_var_p"), sem("var_eps_p"), sem("pow_p"), sem("inv_std_p")
        s_xn, s_xT, s_xh, s_xl = sem("xn_p"), sem("xnT_psum"), sem("xnT_hi"), sem("xnT_lo")
        s_ch, s_cl, s_q, s_k, s_v = sem("cT_hi"), sem("cT_lo"), sem("q_psum"), sem("k_psum"), sem("v_psum")
        s_qh, s_ql, s_kh, s_kl = sem("q_hi"), sem("q_lo"), sem("k_hi"), sem("k_lo")
        s_vh, s_vr, s_vm, s_vl = sem("v_high"), sem("v_rest"), sem("v_mid"), sem("v_low")
        s_s, s_mx, s_ex, s_t, s_ph, s_pl, s_pv = (sem("scores"), sem("neg_max"), sem("exps"), sem("probT"),
                                                  sem("probT_hi"), sem("probT_lo"), sem("pv"))
        s_os, s_on, s_oT, s_oh, s_ol, s_o, s_x2 = (sem("o_sum"), sem("o_norm"), sem("oT"), sem("oT_hi"), sem("oT_lo"),
                                                   sem("wo_out"), sem("residual"))
        s_mv2, s_ve2, s_rs2, s_xn2, s_xT2 = (sem("mean_var_f"), sem("var_eps_f"), sem("inv_std_f"),
                                                    sem("xn_f"), sem("xnT_f"))
        s_fh, s_fl, s_fh2, s_fl2 = sem("ffnT_hi_tile"), sem("ffnT_lo_tile"), sem("ffnT_hi"), sem("ffnT_lo")
        s_gz, s_nz, s_ez, s_rt, s_w, s_wT, s_wTs = (sem("gate_psum"), sem("neg_z"), sem("exp_neg_z"), sem("route_step"),
                                                    sem("weight"), sem("weightT_psum"), sem("weightT"))
        s_bdp, s_bds, s_first = sem("bd_psum"), sem("bd_term"), sem("shared_and_bias")
        s_u, s_ge, s_ah, s_al, s_y, s_ys, s_add, s_moeT, s_res = (
            sem("up"), sem("gelu"), sem("act_hi"), sem("act_lo"), sem("down"), sem("y_scaled"), sem("moe_add"),
            sem("moeT"), sem("result"))

        def wait(engine, semaphore, value):
            if not (isinstance(value, int) and value <= 0):
                engine.wait_ge(semaphore, value)

        def at(i, size):
            return bass.ds(i * size, size)

        def for_groups(engine, step, steps):
            for u in range(steps):
                step(0, u, True)
            with engine.Fori(1, NG - 1) as i:
                for u in range(steps):
                    step(i, u, True)
            for u in range(steps):
                step(NG - 1, u, False)

        def load_k_part(engine, j, h, c, loaded):
            for n in range(HU):
                src = qk_dram[2 + PARTS[c][1], :, bass.ds(j * TOK + h * 2 * SEQ, 2 * SEQ)].rearrange(
                    "(g n d) t -> n d g t", g=UB, n=HU)[n]
                p = DH * (HU * c + n)
                engine.dma_start(k_pack[p:p + DH, h, :, n, :].bitcast(f32), src).then_inc(loaded, 16)

        per_group = 2 * E1 // (NG - 1)

        def y_bank(e):
            return bank[7] if e == E else bank[4 + e % 2]

        def token_tile(i, t):
            return x[:, at(i * GB + t, 1), :].rearrange("p a d -> p (a d)")

        def norm_apply(i, scale, done, tiles):
            for t in tiles:
                nc.vector.tensor_scalar(xn[:, t, :], token_tile(i, t), mean_var[:, t, 0:1], scale[:, t:t + 1],
                                     ALU.subtract, ALU.mult).then_inc(done, 1)

        block = ctx.enter_context(nc.Block())

        @block.sync
        def _(sp):
            xv = x_in.rearrange("b p d -> p b d")
            sp.dma_start(x[:, 0:GB, :], xv[:, 0:GB, :]).then_inc(s_x0, 16)
            sp.dma_start(ctxT[:, 0:TOK], ctxT_in[:, 0:TOK]).then_inc(s_c0, 16)
            sp.dma_start(wqkvo[:, :], wqkvo_in).then_inc(s_wa, 16)
            sp.dma_start(identf[:, :], ident_in).then_inc(s_ident, 16)
            sp.dma_start(mask8[:, :], mask_in).then_inc(s_mask, 16)
            sp.dma_start(gates[:, 0:1], g_x_in.partition_broadcast(128)).then_inc(s_small, 16)
            sp.dma_start(gates[:, 1:2], g_f_in.partition_broadcast(128)).then_inc(s_small, 16)
            sp.dma_start(earlier[:, :], earlier_in.partition_broadcast(128)).then_inc(s_small, 16)
            sp.dma_start(gate_b[:, :], gate_b_in.partition_broadcast(128)).then_inc(s_small, 16)
            sp.dma_start(gate_w[:, :], gate_wT_in).then_inc(s_small, 16)
            sp.dma_start(bu[:, :], bu_in).then_inc(s_small, 16)
            sp.dma_start(bd[:, :], bd_in).then_inc(s_small, 16)
            sp.dma_start(x[:, GB:NB, :], xv[:, GB:NB, :]).then_inc(s_xrest, 16)
            sp.dma_start(ctxT[:, TOK:NB * SEQ], ctxT_in[:, TOK:NB * SEQ]).then_inc(s_xrest, 16)

            def load_w(n, k):
                sp.dma_start(w_raw[:, k:k + 1, :], wffn_in[:, bass.ds(n, 1), :]).then_inc(s_wraw[k], 16)

            def reload_w(j, m):
                for k in range(2):
                    n = per_group * (j - 1) + m + k
                    sp.wait_ge(s_wl, n + 1)
                    load_w(n + 2, k)

            for k in range(2):
                load_w(k, k)

            def store_k(j):
                sp.wait_ge(s_kl, j + 1)
                sp.dma_start(qk_dram[2:4, :, at(j, TOK)].rearrange("a r t -> r a t"),
                             k_parts.bitcast(f32)).then_inc(s_k_out, 16)

            def store_q(j):
                sp.wait_ge(s_ql, j + 1)
                for part, tile in ((1, q_lo), (0, q_hi)):
                    sp.dma_start(qk_dram[part, :, at(j, TOK)], tile.bitcast(f32)).then_inc(s_q_out, 16)

            def load_k(j, h):
                for c in range(len(PARTS)):
                    load_k_part(sp, j, h, c, s_kpack[h])

            def load_q(j, h):
                first = j * TOK + h * 2 * SEQ
                for c, (part, _) in enumerate(PARTS):
                    src = qk_dram[part, :, bass.ds(first, 2 * SEQ)].rearrange("(g r) t -> r g t", g=UB)
                    p = HU * DH * c
                    sp.dma_start(q_pack[p:p + HU * DH, h, :, :].bitcast(f32), src).then_inc(s_qpack[h], 16)

            store_k(0)
            store_q(0)
            sp.wait_ge(s_k_out, 16)
            sp.wait_ge(s_kzero, 1)
            for c in range(len(PARTS) - 1):
                load_k_part(sp, 0, 0, c, s_kpack[0])
            sp.wait_ge(s_q_out, 32)
            load_q(0, 0)
            sp.wait_ge(s_kzero, 2)
            load_q(0, 1)
            load_k(0, 1)

            def beside_group(j, more):
                store_k(j)
                reload_w(j, 0)
                store_q(j)
                sp.wait_ge(s_k_out, 16 * (j + 1))
                sp.wait_ge(s_s, UN * (j - 1) + UN // 2)
                load_k(j, 0)
                sp.wait_ge(s_q_out, 32 * (j + 1))
                load_q(j, 0)
                reload_w(j, 2)
                sp.wait_ge(s_s, UN * j)
                load_k(j, 1)
                load_q(j, 1)
                if more:
                    reload_w(j, 4)

            with sp.Fori(1, NG - 1) as j:
                beside_group(j, True)
            beside_group(NG - 1, False)
            sp.wait_ge(s_s, NG * UN - UN // 2)

            def weights_round(j):
                sp.wait_ge(s_wTs, j + 1)
                sp.dma_start(w_dram[bass.ds(j, 1), :, :].rearrange("a e t -> (a e) t"),
                             weightT[1:E1, :]).then_inc(s_wt_out, 16)
                sp.wait_ge(s_wt_out, 16 * (j + 1))
                for e in range(E):
                    wait(sp, s_ys, E * (j - 1) + e + 1)
                    src = w_dram[bass.ds(j, 1), e, :].rearrange("a t -> (a t)").partition_broadcast(128)
                    sp.dma_start(weight_all[:, e, :], src).then_inc(s_wall, 16)

            weights_round(0)
            with sp.Fori(1, NG) as j:
                weights_round(j)
                sp.wait_ge(s_res, j)
                sp.dma_start(out_dram[at(j - 1, GB), :, :].rearrange("b p d -> p b d"), result[:, :, :]).then_inc(s_out, 16)
            sp.wait_ge(s_res, NG)
            sp.dma_start(out_dram[NB - GB:NB, :, :].rearrange("b p d -> p b d"), result[:, :, :]).then_inc(s_out, 16)
            sp.wait_ge(s_out, 16 * (NG + 1))

        @block.gpsimd
        def _(pool):
            g = nc.gpsimd
            g.memset(minus_half[:, :], -0.5).then_inc(s_pool0, 1)
            g.memset(k_pack[:, 0, :, :, :].bitcast(f32), 0.0).then_inc(s_kzero, 1)
            g.memset(v_parts[:, :, :, VC - 1:VC], 1.0).then_inc(s_pool0, 1)
            g.memset(ones[:, :], 1.0).then_inc(s_pool0, 1)
            g.memset(e_const[:, :], float(np.e)).then_inc(s_pool0, 1)
            g.memset(weight[:, :, 0:1], SHARED_WEIGHT).then_inc(s_pool0, 1)
            g.memset(top_sum[:, :], 0.0).then_inc(s_out, 16)
            pool.wait_ge(s_pool0, 5)
            pool.wait_ge(s_mk, 1)

            def context_low(j):
                pool.wait_ge(s_ch, j + 1)
                g.tensor_tensor(cT_lo, ctxT[:, at(j, TOK)], cT_hi.bitcast(f32), ALU.subtract).then_inc(s_cl, 1)

            def norm_scale(j):
                pool.wait_ge(s_ve, j + 1)
                g.tensor_tensor(inv_std[:, :], var_eps[:, :], minus_half[:, :], ALU.pow).then_inc(s_pw, 1)
                pool.wait_ge(s_pw, j + 1)
                g.tensor_tensor(inv_std_open[:, :], inv_std[:, :], row_open[:, 0:1].broadcast_to([128, GB]),
                                ALU.mult).then_inc(s_rs, 1)

            def normalize_tokens(j):
                shape = [128, GB, D]
                pool.wait_ge(s_rs, j + 1)
                pool.wait_ge(s_xT, j)
                g.tensor_tensor(xn[:, :, :], x[:, at(j, GB), :], mean_var[:, :, 0:1].broadcast_to(shape),
                                ALU.subtract).then_inc(s_xc, 1)
                pool.wait_ge(s_xc, j)
                g.tensor_tensor(xn[:, :, :], xn[:, :, :],
                                inv_std_open[:, :].rearrange("p (t a) -> p t a", a=1).broadcast_to(shape),
                                ALU.mult).then_inc(s_xn, GB)

            def rows(a, n=TOK // DH):
                return a.rearrange("p (n d) -> p n d", n=n)

            def v_rounds(j):
                high = v_parts[:, at(j, GB), :, 0:DH].rearrange("p b h d -> p (b h) d")
                mid = v_parts[:, at(j, GB), :, DH:2 * DH].rearrange("p b h d -> p (b h) d")
                low = v_parts[:, at(j, GB), :, 2 * DH:3 * DH].rearrange("p b h d -> p (b h) d")
                pool.wait_ge(s_vh, 2 * j + 2)
                g.tensor_tensor(rows(wqkvo[:, :]), rows(wqkvo[:, :]), high, ALU.subtract).then_inc(s_vr, 1)
                pool.wait_ge(s_vr, j + 1)
                g.tensor_tensor(mid, rows(wqkvo[:, :]), rows(ones[:, :]), ALU.mult).then_inc(s_vm, 1)
                pool.wait_ge(s_vm, j + 1)
                g.tensor_tensor(low, rows(wqkvo[:, :]), mid, ALU.subtract).then_inc(s_vl, 1)

            def split_w(n, k, uses):
                pool.wait_ge(s_wraw[k], 16 * uses)
                hi, lo = w_hi[:, bass.ds(n, 1), :], w_lo[:, bass.ds(n, 1), :]
                g.tensor_tensor(hi, w_raw[:, k:k + 1, :], ones[:, :].rearrange("p (a n) -> p a n", a=1),
                                ALU.mult).then_inc(s_wh, 1)
                pool.wait_ge(s_wh, n + 1)
                g.tensor_tensor(lo, w_raw[:, k:k + 1, :], hi.bitcast(f32), ALU.subtract).then_inc(s_wl, 1)

            def split_beside(k):
                for m in range(per_group):
                    if m == 4:
                        v_rounds(k + 1)
                    n = k * per_group + m
                    split_w(n, m % 2, k * (per_group // 2) + m // 2 + 1)

            norm_scale(0)
            context_low(0)
            g.memset(k_pack[:, 1, :, :, :].bitcast(f32), 0.0).then_inc(s_kzero, 1)
            pool.wait_ge(s_k_out, 16)
            load_k_part(pool, 0, 0, len(PARTS) - 1, s_kpack_first)
            v_rounds(0)
            with pool.Fori(0, NG - 2) as k:
                context_low(k + 1)
                norm_scale(k + 1)
                normalize_tokens(k + 1)
                split_beside(k)
            context_low(NG - 1)
            norm_scale(NG - 1)
            normalize_tokens(NG - 1)
            split_beside(NG - 2)

            def inverse_std(j):
                pool.wait_ge(s_ve2, j + 1)
                g.tensor_tensor(inv_std[:, :], var_eps[:, :], minus_half[:, :], ALU.pow).then_inc(s_rs2, 1)

            def exp_gate(j):
                pool.wait_ge(s_nz, j + 1)
                g.tensor_tensor(exp_neg_z[:, :, :], e_const[:, :].rearrange("p (t e) -> p t e", t=GB), neg_z[:, :, :],
                                ALU.pow).then_inc(s_ez, 1)

            def add(i, e):
                pool.wait_ge(s_ys, E * i + e)
                wait(pool, s_add, E * i + e - 1)
                if e == 1:
                    pool.wait_ge(s_first, i + 1)
                g.tensor_tensor(moe[:, :], moe[:, :], y_scaled[:, e % 2, :], ALU.add).then_inc(s_add, 1)

            def stage_f(i, more):
                if more:
                    inverse_std(i + 1)
                for e in range(1, E1):
                    add(i, e)
                    if more and e == 3:
                        exp_gate(i + 1)

            inverse_std(0)
            exp_gate(0)
            stage_f(0, True)
            with pool.Fori(1, NG - 1) as i:
                stage_f(i, True)
            stage_f(NG - 1, False)

        @block.scalar
        def _(act_e):
            a = nc.scalar
            def context_high(j):
                if not isinstance(j, int) or j:
                    act_e.wait_ge(s_xrest, 32)
                else:
                    act_e.wait_ge(s_c0, 16)
                wait(act_e, s_v, j)
                a.activation(cT_hi, ctxT[:, at(j, TOK)], ACT.Copy).then_inc(s_ch, 1)

            def k_high(j, bk):
                act_e.wait_ge(s_k, j + 1)
                wait(act_e, s_k_out, 16 * j)
                a.activation(k_hi, bk[:, :], ACT.Copy).then_inc(s_kh, 1)

            def xn_high(j, bk):
                act_e.wait_ge(s_xT, j + 1)
                a.activation(xnT_hi[:, :], bk[:, :], ACT.Copy).then_inc(s_xh, 1)

            def v_high(j, bk):
                act_e.wait_ge(s_v, j + 1)
                wait(act_e, s_vl, j)
                a.activation(v_rest, bk[:, :], ACT.Copy).then_inc(s_vh, 1)
                a.activation(v_parts[:, at(j, GB), :, 0:DH],
                             bk[:, :].rearrange("p (b h d) -> p b h d", b=GB, h=HEADS), ACT.Copy).then_inc(s_vh, 1)

            def q_high(j, bk):
                act_e.wait_ge(s_q, j + 1)
                wait(act_e, s_q_out, 32 * j)
                a.activation(q_hi, bk[:, :], ACT.Copy, scale=QSCALE).then_inc(s_qh, 1)

            context_high(0)
            act_e.wait_ge(s_wa, 16)
            a.activation(wqkvo_hi[:, :], wqkvo[:, :], ACT.Copy).then_inc(s_wah, 1)
            k_high(0, bank[2])
            xn_high(0, bank[0])
            q_high(0, bank[1])
            act_e.wait_ge(s_wal, 1)
            v_high(0, bank[3])

            act_e.wait_ge(s_small, 16 * 7)
            a.activation(tanh_gates[:, :], gates[:, :], ACT.Tanh).then_inc(s_tanh, 1)
            a.activation(gate_hi[:, :], gate_w[:, :], ACT.Copy).then_inc(s_tanh, 1)

            def exps(n, u):
                act_e.wait_ge(s_mx, n + 1)
                wait(act_e, s_t, n - 1)
                for j in range(HU):
                    last = a.activation(prob[:, u % 2, j, :], bank[u % 4][:, SEQ * j:SEQ * (j + 1)], ACT.Exp,
                                        bias=neg_max[:, u % 4, j:j + 1])
                last.then_inc(s_ex, 1)

            def step(i, u, more):
                if u + 1 < UN or more:
                    exps(UN * i + u + 1, (u + 1) % UN)
                if more and u == 9:
                    v_high(i + 1, bank[7])
                n = UN * i + u
                act_e.wait_ge(s_t, n + 1)
                wait(act_e, s_pv, n - 1)
                a.activation(probT_hi[:, u % 2, :], bank[4 + u % 2][:, :], ACT.Copy).then_inc(s_ph, 1)
                if u % UB == 2:
                    high_o(GB * i + u // UB - 1, (u // UB - 1) % 2)
                if more:
                    if u == 0:
                        context_high(i + 1)
                    if u == 1:
                        k_high(i + 1, bank[7])
                    if u == 4:
                        xn_high(i + 1, bank[7])
                    if u == 5:
                        q_high(i + 1, bank[7])
                else:
                    if u == 4:
                        tile_high(0, bank[7])
                    if u == 7:
                        keep_parts(0)
                    if u == 13:
                        weight_rows(0)

            def high_o(b, par):
                if isinstance(b, int) and b < 0:
                    return
                act_e.wait_ge(s_oT, b + 1)
                wait(act_e, s_o, b - 1)
                a.activation(oT_hi[:, par, :], bank[7][:, 0:SEQ], ACT.Copy).then_inc(s_oh, 1)

            def tile_high(j, bk):
                act_e.wait_ge(s_xT2, j + 1)
                wait(act_e, s_gz, j)
                a.activation(xnT_hi[:, :], bk[:, :], ACT.Copy).then_inc(s_fh, 1)

            def keep_parts(j):
                act_e.wait_ge(s_fh, j + 1)
                a.activation(ffnT_hi[:, at(j, TOK)], xnT_hi[:, :].bitcast(f32), ACT.Copy).then_inc(s_fh2, 1)
                act_e.wait_ge(s_fl, j + 1)
                a.activation(ffnT_lo[:, at(j, TOK)], xnT_lo[:, :].bitcast(f32), ACT.Copy).then_inc(s_fl2, 1)

            def weight_rows(j):
                act_e.wait_ge(s_wT, j + 1)
                wait(act_e, s_wt_out, 16 * j)
                wait(act_e, s_bdp, j)
                a.activation(weightT[:, :], bank[7][0:E1, :], ACT.Copy).then_inc(s_wTs, 1)

            exps(0, 0)
            for_groups(act_e, step, UN)

            def bias_term(i):
                act_e.wait_ge(s_bdp, i + 1)
                wait(act_e, s_first, i)
                a.activation(bias_sum, bank[6][:, :], ACT.Copy).then_inc(s_bds, 1)

            def ffn_step(i, n, more):
                m = CH * i + n
                act_e.wait_ge(s_u, m + 1)
                wait(act_e, s_al, m - 3)
                a.activation(act[:, n % 4, :], bank[n % 4][:, :], ACT.Gelu, bias=bu[:, n:n + 1]).then_inc(s_ge, 1)
                if isinstance(i, int) and i == 0 and n == 0:
                    high_o(NB - 1, 1)
                if n:
                    high_act(m - 1, n - 1)
                if n == CH - 1:
                    high_act(m, n)
                if n == 4:
                    bias_term(i)
                if more and n == 12:
                    tile_high(i + 1, bank[6])
                if more and n == 18:
                    keep_parts(i + 1)
                if more and n == 32:
                    weight_rows(i + 1)

            def high_act(m, n):
                act_e.wait_ge(s_ge, m + 1)
                wait(act_e, s_y, m - 3)
                a.activation(act_hi[:, n % 4, :], act[:, n % 4, :], ACT.Copy).then_inc(s_ah, 1)

            for_groups(act_e, ffn_step, CH)

        @block.vector
        def _(dve):
            v = nc.vector
            def norm_stats(i, tiles):
                for t in tiles:
                    v.bn_stats(stats[:, t, :], token_tile(i, t))

            def norm_mean(i, smv, sve):
                dve.drain()
                for t in range(GB):
                    v.bn_aggr(mean_var[:, t, :], stats[:, t, :]).then_inc(smv, 1)
                dve.wait_ge(smv, GB * i + GB)
                v.tensor_scalar(var_eps[:, :], mean_var[:, :, 1], EPS, None, ALU.add).then_inc(sve, 1)

            def k_low(j, bk):
                dve.wait_ge(s_kh, j + 1)
                v.tensor_tensor(k_lo, bk[:, :], k_hi.bitcast(f32), ALU.subtract).then_inc(s_kl, 1)

            def xn_low(j, bk):
                dve.wait_ge(s_xh, j + 1)
                v.tensor_tensor(xnT_lo[:, :], bk[:, :], xnT_hi[:, :].bitcast(f32), ALU.subtract).then_inc(s_xl, 1)

            def q_low(j, bk):
                dve.wait_ge(s_qh, j + 1)
                v.scalar_tensor_tensor(q_lo, bk[:, :], QSCALE, q_hi.bitcast(f32), ALU.mult,
                                       ALU.subtract).then_inc(s_ql, 1)

            dve.wait_ge(s_x0, 16)
            norm_stats(0, range(GB))
            norm_mean(0, s_mv, s_ve)
            dve.wait_ge(s_mask, 16)
            v.tensor_copy(maskf[:, :], mask8[:, :]).then_inc(s_ib, 1)
            dve.wait_ge(s_ib, 1)
            v.reduce_max(row_open[:, :], maskf[:, :], AX.X).then_inc(s_mk, 1)
            v.tensor_scalar(mask_low[:, :], maskf[:, :], 1.0, MASKED, ALU.subtract, ALU.mult).then_inc(s_ib, 1)
            dve.wait_ge(s_mk, 1)
            dve.wait_ge(s_ib, 2)
            v.tensor_scalar(mask_bias[:, :], mask_low[:, :], row_open[:, 0:1], None, ALU.mult).then_inc(s_mk, 1)
            dve.wait_ge(s_wah, 1)
            v.tensor_tensor(wqkvo_lo[:, :], wqkvo[:, :], wqkvo_hi[:, :].bitcast(f32), ALU.subtract).then_inc(s_wal, 1)
            dve.wait_ge(s_ident, 16)
            v.tensor_copy(identb[:, :], identf[:, :]).then_inc(s_ib, 1)
            dve.wait_ge(s_rs, 1)
            norm_apply(0, inv_std_open, s_xn, range(GB))
            k_low(0, bank[2])
            xn_low(0, bank[0])
            q_low(0, bank[1])
            dve.wait_ge(s_xrest, 32)
            dve.wait_ge(s_tanh, 2)
            v.tensor_tensor(gate_lo[:, :], gate_w[:, :], gate_hi[:, :].bitcast(f32), ALU.subtract).then_inc(s_wal, 1)

            def maxima(n, u):
                dve.wait_ge(s_s, n + 1)
                v.tensor_reduce(neg_max[:, u % 4, :], bank[u % 4][:, :].rearrange("p (j k) -> p j k", j=HU), AX.X,
                                ALU.max, negate=True).then_inc(s_mx, 1)

            def normalize(b, par):
                if isinstance(b, int) and b < 0:
                    return
                dve.wait_ge(s_pv, UB * b + UB)
                o = bank[6][:, 0:HEADS * VC].rearrange("p (h c) -> p h c", c=VC)
                v.tensor_reduce(o_sum[:, :, :], o[:, :, 0:3 * DH].rearrange("p h (c d) -> p h d c", c=3), AX.X,
                                ALU.add).then_inc(s_os, 1)
                v.reciprocal(inv_sum[:, :], o[:, :, VC - 1]).then_inc(s_os, 1)
                dve.wait_ge(s_os, 2 * b + 2)
                v.tensor_tensor(o_norm[:, par, :, :], o_sum[:, :, :],
                                inv_sum[:, :].rearrange("p (h a) -> p h a", a=1).broadcast_to([128, HEADS, DH]),
                                ALU.mult).then_inc(s_on, 1)

            def low_o(b, par):
                if isinstance(b, int) and b < 0:
                    return
                dve.wait_ge(s_oh, b + 1)
                v.tensor_tensor(oT_lo[:, par, :], bank[7][:, 0:SEQ], oT_hi[:, par, :].bitcast(f32),
                                ALU.subtract).then_inc(s_ol, 1)

            def residual(b, par):
                if isinstance(b, int) and b < 0:
                    return
                dve.wait_ge(s_o, b + 1)
                xb = x[:, at(b, 1), :].rearrange("p a d -> p (a d)")
                v.scalar_tensor_tensor(xb, bank[7][:, SEQ:SEQ + D], tanh_gates[:, 0:1], xb, ALU.mult,
                                       ALU.add).then_inc(s_x2, 1)

            def step(i, u, more):
                if u + 2 < UN or more:
                    maxima(UN * i + u + 2, (u + 2) % UN)
                n = UN * i + u
                dve.wait_ge(s_ph, n + 1)
                v.tensor_tensor(probT_lo[:, u % 2, :], bank[4 + u % 2][:, :], probT_hi[:, u % 2, :],
                                ALU.subtract).then_inc(s_pl, 1)
                b, par = GB * i + u // UB - 1, (u // UB - 1) % 2
                if u % UB == 2:
                    low_o(b, par)
                if u % UB == 3:
                    residual(b, par)
                if u == 4:
                    if more:
                        xn_low(i + 1, bank[7])
                    else:
                        xn_parts(0, bank[7])
                if u % UB == 0:
                    normalize(b, par)
                if more:
                    if u == 0:
                        norm_stats(i + 1, range(GB))
                    if u == 1:
                        norm_mean(i + 1, s_mv, s_ve)
                        k_low(i + 1, bank[7])
                    if u == 5:
                        q_low(i + 1, bank[7])
                else:
                    if u == 0:
                        norm_stats(0, (0, 1))
                    if u == 1:
                        norm_stats(0, (2, 3))
                        norm_mean(0, s_mv2, s_ve2)
                    if u == 2:
                        dve.wait_ge(s_rs2, 1)
                        norm_apply(0, inv_std, s_xn2, range(GB))
                    if u == 5:
                        gate_logits(0)
                    if u == 9:
                        dve.wait_ge(s_vl, NG)
                        route(0, 0)
                    if 9 <= u < 13:
                        route(0, u - 8)

            def xn_parts(j, bk):
                dve.wait_ge(s_fh, j + 1)
                v.tensor_tensor(xnT_lo[:, :], bk[:, :], xnT_hi[:, :].bitcast(f32), ALU.subtract).then_inc(s_fl, 1)

            def gate_logits(j):
                dve.wait_ge(s_gz, j + 1)
                v.scalar_tensor_tensor(neg_z[:, :, :], bank[7][:, 0:GB * E].rearrange("p (t e) -> p t e", t=GB), -1.0,
                                       gate_b[:, :].rearrange("p (a e) -> p a e", a=1).broadcast_to([128, GB, E]),
                                       ALU.mult, ALU.subtract).then_inc(s_nz, 1)

            def route(j, part):
                steps = 9
                if part == 0:
                    dve.wait_ge(s_ez, j + 1)
                    v.tensor_scalar(sig_den[:, :, :], exp_neg_z[:, :, :], 1.0, None, ALU.add).then_inc(s_rt, 1)
                    dve.wait_ge(s_rt, steps * j + 1)
                    v.reciprocal(sig[:, :, :], sig_den[:, :, :]).then_inc(s_rt, 1)
                if part == 1:
                    dve.wait_ge(s_rt, steps * j + 2)
                    this = sig[:, :, :].rearrange("p t (e a) -> p t e a", a=1).broadcast_to([128, GB, E, E])
                    other = sig[:, :, :].rearrange("p t (a e) -> p t a e", a=1).broadcast_to([128, GB, E, E])
                    v.tensor_tensor(beats[:, :, :, :], other, this, ALU.is_gt).then_inc(s_rt, 1)
                    v.tensor_tensor(ties[:, :, :, :], other, this, ALU.is_equal).then_inc(s_rt, 1)
                    dve.wait_ge(s_rt, steps * j + 4)
                    flat = ties[:, :, :, :].rearrange("p t e f -> p t (e f)")
                    before = earlier[:, :].rearrange("p (a n) -> p a n", a=1).broadcast_to([128, GB, E * E])
                    v.tensor_tensor(flat, flat, before, ALU.mult).then_inc(s_rt, 1)
                if part == 2:
                    dve.wait_ge(s_rt, steps * j + 5)
                    v.tensor_tensor(beats[:, :, :, :], beats[:, :, :, :], ties[:, :, :, :], ALU.add).then_inc(s_rt, 1)
                    dve.wait_ge(s_rt, steps * j + 6)
                    v.tensor_reduce(rank[:, :, :], beats[:, :, :, :], AX.X, ALU.add).then_inc(s_rt, 1)
                if part == 3:
                    dve.wait_ge(s_rt, steps * j + 7)
                    v.scalar_tensor_tensor(sig_top[:, :, :], rank[:, :, :], 2.0, sig[:, :, :], ALU.is_lt,
                                           ALU.mult).then_inc(s_rt, 1)
                    dve.wait_ge(s_rt, steps * j + 8)
                    v.tensor_reduce(top_sum[:, :], sig_top[:, :, :], AX.X, ALU.add).then_inc(s_rt, 1)
                    dve.wait_ge(s_rt, steps * j + 9)
                    v.tensor_scalar(top_sum[:, :], top_sum[:, :], TINY, None, ALU.add).then_inc(s_w, 1)
                if part == 4:
                    dve.wait_ge(s_w, 3 * j + 1)
                    v.reciprocal(inv_top[:, :], top_sum[:, :]).then_inc(s_w, 1)
                    dve.wait_ge(s_w, 3 * j + 2)
                    wait(dve, s_wT, j)
                    v.tensor_tensor(weight[:, :, 1:E1], sig_top[:, :, :],
                                    inv_top[:, :].rearrange("p (t a) -> p t a", a=1).broadcast_to([128, GB, E]),
                                    ALU.mult).then_inc(s_w, 1)

            maxima(0, 0)
            maxima(1, 1)
            for_groups(dve, step, UN)
            normalize(NB - 1, 1)
            low_o(NB - 1, 1)
            residual(NB - 1, 1)

            def combine(i, e):
                dve.wait_ge(s_y, CH * i + FC * e + FC)
                y = y_bank(e)
                if e == 0:
                    dve.wait_ge(s_bds, i + 1)
                    wait(dve, s_moeT, i)
                    v.scalar_tensor_tensor(moe[:, :], y[:, :], SHARED_WEIGHT, bias_sum, ALU.mult,
                                           ALU.add).then_inc(s_first, 1)
                else:
                    dve.wait_ge(s_wall, 16 * (E * i + E))
                    wait(dve, s_add, E * i + e - 2)
                    v.tensor_tensor(y_scaled[:, e % 2, :], y[:, :], weight_all[:, e - 1, :], ALU.mult).then_inc(s_ys, 1)

            def finish(i):
                if isinstance(i, int) and i < 0:
                    return
                dve.wait_ge(s_moeT, i + 1)
                dve.wait_ge(s_out, 16 * (i + 1))
                v.scalar_tensor_tensor(result[:, :, :], bank[7][:, :].rearrange("p (b d) -> p b d", b=GB),
                                       tanh_gates[:, 1:2], x[:, at(i, GB), :], ALU.mult, ALU.add).then_inc(s_res, 1)

            def ffn_step(i, n, more):
                m = CH * i + n
                dve.wait_ge(s_ah, m + 1)
                wait(dve, s_y, m - 3)
                v.tensor_tensor(act_lo[:, n % 4, :], act[:, n % 4, :], act_hi[:, n % 4, :].bitcast(f32),
                                ALU.subtract).then_inc(s_al, 1)
                if n == 8:
                    combine(i, 0)
                if n % FC == 1 and n > 2 * FC:
                    combine(i, n // FC - 1)
                if n == 7:
                    finish(i - 1)
                if n == 2 and not (isinstance(i, int) and i == 0):
                    combine(i - 1, E)
                if more and n == 1:
                    norm_stats(i + 1, (0, 1))
                if more and n == 2:
                    norm_stats(i + 1, (2, 3))
                if more and n == 3:
                    norm_mean(i + 1, s_mv2, s_ve2)
                if more and n == 5:
                    dve.wait_ge(s_rs2, i + 2)
                    norm_apply(i + 1, inv_std, s_xn2, (0, 1))
                if more and n == 6:
                    norm_apply(i + 1, inv_std, s_xn2, (2, 3))
                if more and n == 14:
                    xn_parts(i + 1, bank[6])
                if more and n == 19:
                    gate_logits(i + 1)
                if more and 25 <= n < 30:
                    route(i + 1, n - 25)

            for_groups(dve, ffn_step, CH)
            combine(NG - 1, E)
            finish(NG - 1)

        @block.tensor
        def _(pe):
            mm = nc.tensor.matmul

            def three(out, w_h, w_l, r_h, r_l, start=True, stop=True):
                mm(out, w_h, r_h, start=start, stop=False)
                mm(out, w_l, r_h, start=False, stop=False)
                return mm(out, w_h, r_l, start=False, stop=stop)

            def wa(part, k):
                return part[:, D * k:D * (k + 1)]

            pe.wait_ge(s_ident, 16)
            pe.wait_ge(s_wah, 1)

            def project_k(j, bk):
                pe.wait_ge(s_cl, j + 1)
                three(bk[:, :], wa(wqkvo_hi, 1), wa(wqkvo_lo, 1), cT_hi, cT_lo).then_inc(s_k, 1)

            def transpose_xn(j, bk):
                pe.wait_ge(s_xn, GB * j + GB)
                for t in range(GB):
                    last = nc.tensor.transpose(bk[:, D * t:D * (t + 1)], xn[:, t, :], identf[:, :])
                last.then_inc(s_xT, 1)

            def project_v(j, bk):
                for t in range(GB):
                    c = slice(SEQ * t, SEQ * (t + 1))
                    last = three(bk[:, c], cT_hi[:, c], cT_lo[:, c], wa(wqkvo_hi, 2), wa(wqkvo_lo, 2))
                last.then_inc(s_v, 1)

            def project_q(j, bk):
                pe.wait_ge(s_xl, j + 1)
                three(bk[:, :], wa(wqkvo_hi, 0), wa(wqkvo_lo, 0), xnT_hi[:, :], xnT_lo[:, :]).then_inc(s_q, 1)

            pe.wait_ge(s_wal, 1)
            project_k(0, bank[2])
            transpose_xn(0, bank[0])
            project_q(0, bank[1])
            project_v(0, bank[3])

            def scores(i, u):
                b, g = u // UB, u % UB
                h = b // 2
                if u % (UN // 2) == 0:
                    pe.wait_ge(s_qpack[h], 16 * len(PARTS) * (i + 1))
                    pe.wait_ge(s_kpack[h], 16 * HU * (len(PARTS) * (i + 1) - (1 if h == 0 else 0)))
                out = bank[u % 4]
                t = slice(SEQ * (b % 2), SEQ * (b % 2 + 1))
                out4 = out[:, :].rearrange("p (j k) -> p j k", j=HU)
                mm(out4, q_pack[:, h, g, t], k_pack[0:KR, h, g, :, t], start=True, stop=False)
                mm(out4, identb[:, :],
                   mask_bias[:, :].rearrange("p (a k) -> p a k", a=1).broadcast_to([128, HU, SEQ]),
                   start=False, stop=True).then_inc(s_s, 1)

            def pv(i, u):
                b, g = u // UB, u % UB
                n = UN * i + u
                pe.wait_ge(s_pl, n + 1)
                if u == 0:
                    pe.wait_ge(s_vl, i + 1)
                if g == 0:
                    wait(pe, s_os, 2 * (GB * i + b))
                for j in range(HU):
                    h = HU * g + j
                    out = bank[6][:, VC * h:VC * (h + 1)]
                    rhs = v_parts[:, at(GB * i + b, 1), h, :].rearrange("p a c -> p (a c)")
                    mm(out, probT_hi[:, u % 2, SEQ * j:SEQ * (j + 1)], rhs, start=True, stop=False)
                    last = mm(out, probT_lo[:, u % 2, SEQ * j:SEQ * (j + 1)], rhs, start=False, stop=True)
                last.then_inc(s_pv, 1)

            def o_transpose(b, par):
                if isinstance(b, int) and b < 0:
                    return
                pe.wait_ge(s_on, b + 1)
                wait(pe, s_x2, b)
                nc.tensor.transpose(bank[7][:, 0:SEQ], o_norm[:, par, :, :].rearrange("p h d -> p (h d)"),
                                    identf[:, :]).then_inc(s_oT, 1)

            def wo(b, par):
                if isinstance(b, int) and b < 0:
                    return
                pe.wait_ge(s_ol, b + 1)
                three(bank[7][:, SEQ:SEQ + D], oT_hi[:, par, :], oT_lo[:, par, :], wa(wqkvo_hi, 3),
                      wa(wqkvo_lo, 3)).then_inc(s_o, 1)

            def ffn_transpose(j, bk):
                pe.wait_ge(s_xn2, GB * j + GB)
                wait(pe, s_bds, j)
                for t in range(GB):
                    last = nc.tensor.transpose(bk[:, D * t:D * (t + 1)], xn[:, t, :], identf[:, :])
                last.then_inc(s_xT2, 1)

            def gate(j):
                pe.wait_ge(s_fl, j + 1)
                wait(pe, s_res, j - 1)
                if isinstance(j, int) and j == 1:
                    pe.wait_ge(s_x2, NB)
                for t in range(GB):
                    c = slice(SEQ * t, SEQ * (t + 1))
                    last = three(bank[7][:, E * t:E * (t + 1)], xnT_hi[:, c], xnT_lo[:, c], gate_hi[:, :], gate_lo[:, :])
                last.then_inc(s_gz, 1)

            def weight_transpose(j):
                pe.wait_ge(s_w, 3 * j + 3)
                for t in range(GB):
                    last = nc.tensor.transpose(bank[7][0:E1, SEQ * t:SEQ * (t + 1)], weight[:, t, :], identf[:, :])
                last.then_inc(s_wT, 1)

            def step(i, u, more):
                n = UN * i + u
                wait(pe, s_ex, n)
                if u + 3 < UN:
                    scores(i, u + 3)
                elif more:
                    scores(i + 1, u + 3 - UN)
                pe.wait_ge(s_ex, n + 1)
                wait(pe, s_pl, n - 1)
                for j in range(HU):
                    last = nc.tensor.transpose(bank[4 + u % 2][:, SEQ * j:SEQ * (j + 1)], prob[:, u % 2, j, :],
                                               identf[:, :])
                last.then_inc(s_t, 1)
                b, par = GB * i + u // UB - 1, (u // UB - 1) % 2
                if more:
                    if u == 1:
                        wait(pe, s_x2, b)
                        project_k(i + 1, bank[7])
                    if u == 4:
                        wait(pe, s_x2, b)
                        transpose_xn(i + 1, bank[7])
                    if u == 5:
                        project_q(i + 1, bank[7])
                    if u == 8:
                        wait(pe, s_x2, b)
                        project_v(i + 1, bank[7])
                else:
                    if u == 4:
                        wait(pe, s_x2, b)
                        ffn_transpose(0, bank[7])
                    if u == 5:
                        pe.wait_ge(s_wal, 2)
                        gate(0)
                    if u == 13:
                        wait(pe, s_x2, b)
                        weight_transpose(0)
                if u % UB == 2:
                    if more and u == 2:
                        pe.wait_ge(s_kl, i + 2)
                    if more and u == 6:
                        pe.wait_ge(s_ql, i + 2)
                    if more and u == 10:
                        pe.wait_ge(s_vh, 2 * i + 4)
                    if not more and u == 6:
                        pe.wait_ge(s_nz, 1)
                    if not more and u == 14:
                        pe.wait_ge(s_wTs, 1)
                    o_transpose(b, par)
                if u:
                    pv(i, u - 1)
                elif not (isinstance(i, int) and i == 0):
                    pv(i - 1, UN - 1)
                if u % UB == 3:
                    wo(b, par)

            pe.wait_ge(s_mk, 2)
            pe.wait_ge(s_ib, 3)
            pe.wait_ge(s_vh, 2)
            pe.wait_ge(s_kl, 1)
            pe.wait_ge(s_ql, 1)
            pe.wait_ge(s_pool0, 5)
            pe.wait_ge(s_kpack_first, 16 * HU)
            for u in range(3):
                scores(0, u)
            for_groups(pe, step, UN)

            def bias_term(i):
                pe.wait_ge(s_wTs, i + 1)
                pe.wait_ge(s_fh2, i + 1)
                mm(bank[6][:, :], bd[:, :], weightT[:, :], start=True, stop=True).then_inc(s_bdp, 1)

            def up(i, n):
                m = CH * i + n
                e, c = n // FC, n % FC
                wait(pe, s_ge, m - 3)
                if n == 0:
                    pe.wait_ge(s_fl2, i + 1)
                k = slice(D * c, D * (c + 1))
                three(bank[n % 4][:, :], w_hi[:, e, k], w_lo[:, e, k], ffnT_hi[:, at(i, TOK)],
                      ffnT_lo[:, at(i, TOK)]).then_inc(s_u, 1)

            def down(i, n, more):
                m = CH * i + n
                e, c = n // FC, n % FC
                pe.wait_ge(s_al, m + 1)
                if c == 0:
                    if e < E:
                        wait(pe, s_ys, E * i + e - 2)
                    if e == 2:
                        pe.wait_ge(s_first, i + 1)
                    if e == E and more:
                        pe.wait_ge(s_wTs, i + 2)
                    if e == E and not more:
                        pe.wait_ge(s_res, i)
                k = slice(D * c, D * (c + 1))
                three(y_bank(e)[:, :], w_hi[:, E1 + e, k], w_lo[:, E1 + e, k], act_hi[:, n % 4, :],
                      act_lo[:, n % 4, :], start=(c == 0), stop=(c == FC - 1)).then_inc(s_y, 1)

            def moe_transpose(i):
                if isinstance(i, int) and i < 0:
                    return
                pe.wait_ge(s_add, E * i + E)
                pe.wait_ge(s_wTs, min(NG, i + 2) if isinstance(i, int) else i + 2)
                for t in range(GB):
                    last = nc.tensor.transpose(bank[7][:, D * t:D * (t + 1)], moe[:, SEQ * t:SEQ * (t + 1)], identf[:, :])
                last.then_inc(s_moeT, 1)

            def ffn_step(i, n, more):
                if n + 3 < CH:
                    up(i, n + 3)
                elif more:
                    up(i + 1, n + 3 - CH)
                down(i, n, more)
                if n == 4:
                    moe_transpose(i - 1)
                if more and n == 8:
                    ffn_transpose(i + 1, bank[6])
                if more and n == 15:
                    gate(i + 1)
                if more and n == 29:
                    weight_transpose(i + 1)
                if n == 0:
                    bias_term(i)

            pv(NG - 1, UN - 1)
            pe.wait_ge(s_wl, 2 * E1)
            pe.wait_ge(s_ex, NG * UN)
            up(0, 0)
            o_transpose(NB - 1, 1)
            up(0, 1)
            wo(NB - 1, 1)
            up(0, 2)
            for_groups(pe, ffn_step, CH)
            moe_transpose(NG - 1)


def kernel(x, ctx_1024, mask_SxS2_bk0, g_xattn, g_ffn, L0_xattn_Wq, L0_xattn_Wk, L0_xattn_Wv, L0_xattn_Wo,
           L0_ffn_gate_w, L0_ffn_gate_bias, L0_ffn_Wu, L0_ffn_bu, L0_ffn_Wd, L0_ffn_bd, L0_ffn_sWu, L0_ffn_sbu,
           L0_ffn_sWd, L0_ffn_sbd):
    import concourse.bacc as bacc
    from concourse.bass_utils import run_bass_kernel_spmd

    def host(a):
        return np.ascontiguousarray(np.asarray(a))

    x = host(x)
    NB, SEQ, D = x.shape
    E, F = host(L0_ffn_bu).shape
    ctxT = host(host(ctx_1024).reshape(NB * SEQ, D).T)
    wqkvo = host(np.stack([host(w).T for w in (L0_xattn_Wq, L0_xattn_Wk, L0_xattn_Wv, L0_xattn_Wo)], 1).reshape(D, 4 * D))
    wu = np.concatenate([host(L0_ffn_sWu)[None], host(L0_ffn_Wu)], 0)
    wd = np.concatenate([host(L0_ffn_sWd)[None], host(L0_ffn_Wd)], 0)
    up = wu.transpose(2, 0, 1)
    down = wd.reshape(E + 1, D, F // 128, 128).transpose(3, 0, 2, 1).reshape(128, E + 1, F)
    wffn = host(np.concatenate([up, down], 1))
    bu = host(np.concatenate([host(L0_ffn_sbu)[None], host(L0_ffn_bu)], 0).reshape(-1, 128).T)
    bd = host(np.concatenate([host(L0_ffn_sbd)[None], host(L0_ffn_bd)], 0))
    arrays = {
        "x_in": x, "ctxT_in": ctxT, "mask_in": host(mask_SxS2_bk0), "g_x_in": host(g_xattn),
        "g_f_in": host(g_ffn), "wqkvo_in": wqkvo, "wffn_in": wffn, "bu_in": bu, "bd_in": bd,
        "gate_wT_in": host(host(L0_ffn_gate_w).T), "gate_b_in": host(L0_ffn_gate_bias),
        "ident_in": np.eye(128, dtype=np.float32),
        "earlier_in": np.tril(np.ones((E, E), np.float32), -1).reshape(-1),
    }
    nc = bacc.Bacc("TRN2", target_bir_lowering=False, num_devices=1)
    args = [nc.dram_tensor(n, a.shape, mybir.dt.from_np(a.dtype), kind="ExternalInput").ap() for n, a in arrays.items()]
    out = nc.dram_tensor("out", (NB, SEQ, D), mybir.dt.float32, kind="ExternalOutput").ap()
    build(nc, *args, out)
    r = run_bass_kernel_spmd(nc, [arrays], core_ids=[0])
    return r.results[0]["out"]
```
